# Optimizing a Trainium2 kernel written in Bass

```python
import numpy as np
import jax
import jax.numpy as jnp

def _softmax(x, axis=-1):
    return jax.nn.softmax(x, axis=axis)

def _gelu(x):
    return jax.nn.gelu(x, approximate=True)

def _silu(x):
    return jax.nn.silu(x)

def _sigmoid(x):
    return jax.nn.sigmoid(x)

def _layernorm(x, axis=-1, eps=1e-05):
    m = jnp.mean(x, axis=axis, keepdims=True)
    v = jnp.var(x, axis=axis, keepdims=True)
    return (x - m) / jnp.sqrt(v + eps)

def _scatter_add(tgt, idx, src, axis=0):
    return tgt.at[idx].add(src)

def _segment_sum(src, seg, n):
    return jax.ops.segment_sum(src, seg, n)
kernel_name = 'mk_seq_postln_d1_jaxref_r8_aa1f2b'

def setup_inputs(seed: int=0):
    np.random.seed(seed)
    _w = jnp.asarray

    def _L0_attn_setup():
        import jax, jax.numpy as jnp
        import numpy as np
        B, T, D = (1, 256, 512)
        H, G = (32, 8)
        HD = D // H
        REP = H // G
        KV_DIM = 2 * HD * G
        key = jax.random.key(seed)
        k0, k1, k2, k3 = jax.random.split(key, 4)
        x = jax.random.normal(k0, (B, T, D), dtype=jnp.float32)
        Wq = jax.random.normal(k1, (D, D), dtype=jnp.float32) * 0.02
        Wkv = jax.random.normal(k2, (D, KV_DIM), dtype=jnp.float32) * 0.02
        Wo = jax.random.normal(k3, (D, D), dtype=jnp.float32) * 0.02
        bo = jnp.zeros((D,), dtype=jnp.float32)
        return {'x': x, 'Wq': Wq, 'Wkv': Wkv, 'Wo': Wo, 'bo': bo}
    _L0_attn_in = _L0_attn_setup()

    def _L0_ffn_setup():
        import jax, jax.numpy as jnp
        import numpy as np
        BLOCK = 64
        NF4_CODE = jnp.array([-1.0, -0.6961928009986877, -0.5250730514526367, -0.39491748809814453, -0.28444138169288635, -0.18477343022823334, -0.09105003625154495, 0.0, 0.07958029955625534, 0.16093020141124725, 0.24611230194568634, 0.33791524171829224, 0.44070982933044434, 0.5626170039176941, 0.7229568362236023, 1.0], dtype=jnp.float32)

        def dequant_nf4(q, absmax, shape):
            w = NF4_CODE[q.reshape(-1)]
            w = w.reshape(-1, BLOCK) * absmax[:, None]
            return w.reshape(shape)
        key = jax.random.key(seed)
        ks = jax.random.split(key, 7)
        HD, M = (512, 1792)
        nblk = HD * M // BLOCK
        x = jax.random.normal(ks[0], (2, 256, HD), dtype=jnp.float32)
        gate_q = jax.random.randint(ks[1], (M, HD), 0, 16, dtype=jnp.int32)
        up_q = jax.random.randint(ks[2], (M, HD), 0, 16, dtype=jnp.int32)
        down_q = jax.random.randint(ks[3], (HD, M), 0, 16, dtype=jnp.int32)
        gate_absmax = jax.random.uniform(ks[4], (nblk,), dtype=jnp.float32) * 0.05
        up_absmax = jax.random.uniform(ks[5], (nblk,), dtype=jnp.float32) * 0.05
        down_absmax = jax.random.uniform(ks[6], (nblk,), dtype=jnp.float32) * 0.05
        return {'x': x, 'gate_q': gate_q, 'gate_absmax': gate_absmax, 'up_q': up_q, 'up_absmax': up_absmax, 'down_q': down_q, 'down_absmax': down_absmax}
    _L0_ffn_in = _L0_ffn_setup()
    _d = {'L0_attn_x': _L0_attn_in['x'], 'L0_attn_Wq': _L0_attn_in['Wq'], 'L0_attn_Wkv': _L0_attn_in['Wkv'], 'L0_attn_Wo': _L0_attn_in['Wo'], 'L0_attn_bo': _L0_attn_in['bo'], 'L0_ffn_gate_q': _L0_ffn_in['gate_q'], 'L0_ffn_gate_absmax': _L0_ffn_in['gate_absmax'], 'L0_ffn_up_q': _L0_ffn_in['up_q'], 'L0_ffn_up_absmax': _L0_ffn_in['up_absmax'], 'L0_ffn_down_q': _L0_ffn_in['down_q'], 'L0_ffn_down_absmax': _L0_ffn_in['down_absmax']}
    _x0 = _d['L0_attn_x']
    _d['L0_attn_x'] = jax.random.normal(jax.random.fold_in(jax.random.key(seed), 1), (1, 1024, 512), dtype=_x0.dtype)
    del _x0
    return _d

def reference(L0_attn_x, L0_attn_Wq, L0_attn_Wkv, L0_attn_Wo, L0_attn_bo, L0_ffn_gate_q, L0_ffn_gate_absmax, L0_ffn_up_q, L0_ffn_up_absmax, L0_ffn_down_q, L0_ffn_down_absmax):

    def _L0_attn_ref(x, Wq, Wkv, Wo, bo):
        import jax, jax.numpy as jnp
        import numpy as np
        B, T, D = (1, 256, 512)
        H, G = (32, 8)
        HD = D // H
        REP = H // G
        KV_DIM = 2 * HD * G
        b, t, d = x.shape
        q = jnp.dot(x, Wq).reshape(b, t, H, HD).transpose(0, 2, 1, 3)
        kv = jnp.dot(x, Wkv).reshape(b, t, G, 2, HD).transpose(2, 3, 0, 1, 4)
        k, v = (kv[:, 0], kv[:, 1])
        k = jnp.broadcast_to(k[:, :, None], (G, b, REP, t, HD)).reshape(b, H, t, HD)
        v = jnp.broadcast_to(v[:, :, None], (G, b, REP, t, HD)).reshape(b, H, t, HD)
        scores = jnp.einsum('bhqd,bhkd->bhqk', q, k)
        causal = jnp.triu(jnp.ones((t, t), dtype=bool), 1)
        scores = jnp.where(causal[None, None], -jnp.inf, scores)
        weights = jax.nn.softmax(scores * (1.0 / HD ** 0.5), axis=-1)
        ctx = jnp.einsum('bhqk,bhkd->bhqd', weights, v)
        ctx = ctx.transpose(0, 2, 1, 3).reshape(b, t, d)
        return jnp.dot(ctx, Wo) + bo

    def _L0_ffn_ref(x, gate_q, gate_absmax, up_q, up_absmax, down_q, down_absmax):
        import jax, jax.numpy as jnp
        import numpy as np
        BLOCK = 64
        NF4_CODE = jnp.array([-1.0, -0.6961928009986877, -0.5250730514526367, -0.39491748809814453, -0.28444138169288635, -0.18477343022823334, -0.09105003625154495, 0.0, 0.07958029955625534, 0.16093020141124725, 0.24611230194568634, 0.33791524171829224, 0.44070982933044434, 0.5626170039176941, 0.7229568362236023, 1.0], dtype=jnp.float32)

        def dequant_nf4(q, absmax, shape):
            w = NF4_CODE[q.reshape(-1)]
            w = w.reshape(-1, BLOCK) * absmax[:, None]
            return w.reshape(shape)
        HD = x.shape[-1]
        M = gate_q.shape[0]
        Wg = dequant_nf4(gate_q, gate_absmax, (M, HD))
        Wu = dequant_nf4(up_q, up_absmax, (M, HD))
        Wd = dequant_nf4(down_q, down_absmax, (HD, M))
        g = jnp.einsum('bsh,mh->bsm', x, Wg)
        u = jnp.einsum('bsh,mh->bsm', x, Wu)
        h = jax.nn.silu(g) * u
        return jnp.einsum('bsm,hm->bsh', h, Wd)
    x = L0_attn_x
    x = _layernorm(x + _L0_attn_ref(x, L0_attn_Wq, L0_attn_Wkv, L0_attn_Wo, L0_attn_bo), axis=-1)
    x = _layernorm(x + _L0_ffn_ref(x, L0_ffn_gate_q, L0_ffn_gate_absmax, L0_ffn_up_q, L0_ffn_up_absmax, L0_ffn_down_q, L0_ffn_down_absmax), axis=-1)
    return x

_drawn_inputs = setup_inputs


def setup_inputs(seed=0):
    import zlib

    import numpy as np

    out = dict(_drawn_inputs(seed))
    spreads = {'L0_attn_bo': (0.0, 0.1)}
    factors = {'L0_attn_Wq': 8.0,
     'L0_attn_Wkv': 3.264,
     'L0_attn_Wo': 3.312,
     'L0_ffn_gate_absmax': 3.012,
     'L0_ffn_up_absmax': 3.032,
     'L0_ffn_down_absmax': 3.035}
    for name, (base, spread) in spreads.items():
        noise = np.random.default_rng([zlib.crc32(name.encode()), seed]).standard_normal(out[name].shape)
        drawn = base * np.exp(spread * noise) if base else spread * noise
        out[name] = jnp.asarray(drawn.astype(out[name].dtype))
    for name, factor in factors.items():
        out[name] = (out[name] * factor).astype(out[name].dtype)
    return out
```

```python
from contextlib import ExitStack

import numpy as np

import concourse.bass as bass
import concourse.mybir as mybir

F32, F32R, BF16, I32 = mybir.dt.float32, mybir.dt.float32r, mybir.dt.bfloat16, mybir.dt.int32
ALU, ACT, AX = mybir.AluOpType, mybir.ActivationFunctionType, mybir.AxisListType

P = 128
T, D, H, G = 1024, 512, 32, 8
HD = D // H
REP = H // G
KC = D // P
TT = T // P
HALF, NH = 512, T // 512
M = 1792
MT = M // P
BLOCK = 64
UNIT = 512
UNITS = 3 * MT
EPS = 1e-5
NEG = -3.0e38
SCALE = 1.0 / HD ** 0.5

Q_PART = (0, 0, 0, 1, 1, 2)
K_PART = (0, 1, 2, 0, 1, 0)
STACK = HD * len(Q_PART)
MROW = STACK
STACKM = STACK + 3

CODE = np.array([-1.0, -0.6961928009986877, -0.5250730514526367, -0.39491748809814453,
                 -0.28444138169288635, -0.18477343022823334, -0.09105003625154495, 0.0,
                 0.07958029955625534, 0.16093020141124725, 0.24611230194568634, 0.33791524171829224,
                 0.44070982933044434, 0.5626170039176941, 0.7229568362236023, 1.0], np.float32)
ZERO_AT = 7


def hinges(side, starts):
    def fma(a, u, b):
        return np.float32(np.float64(a) * u + np.float64(b))

    def ulps(v, n):
        return (np.array([v], np.float32).view(np.int32) + np.int32(n)).view(np.float32)[0]

    want = {v: side * CODE[ZERO_AT + side * v] for v in range(1 + (8 if side > 0 else 7))}
    total, terms = {v: np.float32(0) for v in want}, []

    def search(v0):
        pts = [v for v in (v0, v0 + 1) if v in want]
        rest = [np.float64(want[v]) - np.float64(total[v]) for v in pts]
        slope = np.float32(rest[1] - rest[0] if len(pts) == 2 else 2 * rest[0])
        for da in sorted(range(-400, 401), key=abs):
            a = ulps(slope, da)
            for db in range(-3, 4):
                b = ulps(np.float32(rest[0] - np.float64(a) * v0), db) if v0 else np.float32(0)
                if (all(total[v] + max(fma(a, v, b), np.float32(0)) == want[v] for v in pts)
                        and all(fma(a, v, b) <= 0 for v in range(-8, v0))):
                    return a, b
        raise ValueError(v0)

    for v0 in starts:
        a, b = search(v0)
        terms.append((float(side * a), float(b)))
        for v in want:
            total[v] = total[v] + max(fma(a, v, b), np.float32(0))
    return terms


RIGHT, LEFT = hinges(1, (1, 3, 5, 7)), hinges(-1, (0, 2, 4, 6))
R0, R1, R2, R3, L1, L2, L3, L0 = range(8)
NLINE = 7
LINES = RIGHT + LEFT[1:]
SLOPE_L0 = LEFT[0][0]

LEAD = 8
MAX_TILES = [(i, kh, r) for i, kh in [(1, 0), (0, 0), (3, 0), (2, 0), (5, 1), (4, 1), (4, 0), (5, 0), (6, 0),
                                      (7, 0), (7, 1), (6, 1)] for r in range(REP)]
NMAX = len(MAX_TILES)
STEPS = [(qh, kt, pr) for qh in range(NH) for kt in range(4 * (qh + 1)) for pr in range(2)]
NST = len(STEPS)
NPV = NST // 2
EARLY_UNITS = 6


def width(i, kh):
    return min(HALF, (i + 1) * P - kh * HALF)


def q_from(qh, kt):
    return max(qh * HALF, kt * P)


def build_program(nc, t):
    ctx = ExitStack()
    with ctx:
        base = nc.sbuf_base
        base = (base + 63) // 64 * 64

        def at(name, kib, shape, dt):
            return nc.alloc_sbuf_tensor_at(name, shape, dt, offset=base + int(kib * 1024))

        xres = at("xres", 0, [P, TT, D], F32)
        ident_f = at("ident_f", 16, [P, P], F32)
        ident_b = at("ident_b", 16.5, [P, P], BF16)
        mask_q = at("mask_q", 16.75, [P, P], BF16)
        mask_k = at("mask_k", 17, [P, P], BF16)
        row_max = at("row_max", 17.25, [P, 3, 32], F32)
        row_max_hi = at("row_max_hi", 17.625, [P, REP, 4], F32)
        bo_all = at("bo_all", 204, [P, D], F32)
        eps = at("eps", 17.6875, [P, 1], F32)
        ln_stats = at("ln_stats", 17.71875, [P, 2, 6], F32)
        ln_mv = at("ln_mv", 17.78125, [P, 4, 2], F32)
        ln_std = at("ln_std", 17.8125, [P, 4, 1], F32)
        ln_rstd = at("ln_rstd", 17.84375, [P, 4, 1], F32)
        w_down = at("w_down", 18, [P, MT, UNIT], F32)
        codes = at("codes", 46, [P, UNIT], I32)
        scales = at("scales", 48, [P, UNIT], F32)
        u_a = at("u_a", 50, [P, UNIT], BF16)
        lines_a = at("lines_a", 51, [P, 8, UNIT], F32)
        wo_hi = at("wo_hi", 67, [P, KC, D], F32R)
        wo_lo = at("wo_lo", 75, [P, KC, D], F32R)
        xT_raw = at("xT_raw", 83, [P, KC, T], F32)
        w_raw = at("w_raw", 99, [P, KC, 6 * P], F32)
        q_stack = [at(f"q_stack{b}", 83 + 8 * b, [P, REP * T], BF16) for b in range(3)]
        x1T_hi = at("x1T_hi", 83, [P, KC, T], F32R)
        x1T_lo = at("x1T_lo", 99, [P, KC, T], F32R)
        E = 115
        w_hi = at("w_hi", E, [P, KC, 6 * P], F32R)
        w_lo = at("w_lo", E + 12, [P, KC, 6 * P], F32R)
        probs = at("probs", E, [P, 4, 2, HALF], F32)
        ctx_raw = at("ctx_raw", E + 16, [P, NH, HALF], F32)
        ctx_in = at("ctx_in", E + 20, [P, T], F32)
        sum_in = at("sum_in", E + 24, [P, T], F32)
        qk_parts = at("qk_parts", E + 28, [P, 1, 3, HALF], BF16)
        resid = at("resid", E + 31, [P, HALF], F32)
        v_all = at("v_all", E + 33, [P, TT, P], F32)
        v_ones = [at(f"v_ones{b}", E + 37 + b, [P, TT, 32], F32) for b in range(3)]
        k_stack = [at(f"k_stack{b}", E + 40 + 2 * b, [P, T], BF16) for b in range(3)]
        neg_max = at("neg_max", E + 46, [32, 3, P], BF16)
        neg_max_f = at("neg_max_f", E + 46.75, [32, P], F32)
        wo_raw = at("wo_raw", E + 48, [P, KC, D], F32)
        xT_hi = at("xT_hi", E + 56, [P, KC, T], F32R)
        xT_lo = at("xT_lo", E + 72, [P, KC, T], F32R)
        ctx_hi = at("ctx_hi", E + 56, [P, KC, T], F32R)
        ctx_lo = at("ctx_lo", E + 72, [P, KC, T], F32R)
        gu_hi = at("gu_hi", E, [P, 2, 2, UNIT], F32R)
        gu_lo = at("gu_lo", E + 8, [P, 2, 2, UNIT], F32R)
        hid = at("hid", E + 16, [P, MT, T], F32)
        lines_b = at("lines_b", E + 72, [P, 8, UNIT], F32)
        u_b = at("u_b", E + 88, [P, UNIT], BF16)
        wd_hi = at("wd_hi", 46, [P, MT, D], F32R)
        wd_lo = at("wd_lo", 83, [P, MT, D], F32R)
        hid_hi = [at("hid_hi0", E, [P, MT, P], F32R), at("hid_hi1", E + 72, [P, MT, P], F32R)]
        hid_lo = [at("hid_lo0", E + 7, [P, MT, P], F32R), at("hid_lo1", E + 79, [P, MT, P], F32R)]
        lines = [lines_a, lines_b]
        us = [u_a, u_b]

        ps = nc.alloc_psum_tensor("ps", [P, 8, HALF], F32)
        B_MAX, B_CTX, B_TR = 4, 6, 7

        def sem(name):
            return ctx.enter_context(nc.semaphore(name))

        xT_in = [sem(f"xT_in{k}") for k in range(KC)]
        w_in = [sem(f"w_in{k}") for k in range(KC)]
        xres_in, bo_in, wo_in = sem("xres_in"), sem("bo_in"), sem("wo_in")
        consts, k_ones = sem("consts"), sem("k_ones")
        x_hi_s, x_lo_s, w_hi_s, w_lo_s = sem("x_hi_s"), sem("x_lo_s"), sem("w_hi_s"), sem("w_lo_s")
        wo_hi_s, wo_lo_s = sem("wo_hi_s"), sem("wo_lo_s")
        bo_added = sem("bo_added")
        proj = sem("proj")
        part_h, part_r, part_m, parts = sem("part_h"), sem("part_r"), sem("part_m"), sem("parts")
        parts_stored = sem("parts_stored")
        v_ready = sem("v_ready")
        v_staged = sem("v_staged")
        stack_in = [sem(f"stack_in{b}") for b in range(3)]
        max_scores, max_done, max_all, max_T = sem("max_scores"), sem("max_done"), sem("max_all"), sem("max_T")
        nm_h, nm_r, nm_m, nm_all = sem("nm_h"), sem("nm_r"), sem("nm_m"), sem("nm_all")
        mrow_in = sem("mrow_in")
        st_ready, exp_done, pv_done = sem("st_ready"), sem("exp_done"), sem("pv_done")
        ctx_evac = sem("ctx_evac")
        ctx_stored = [sem(f"ctx_stored{h}") for h in range(NH)]
        ctx_loaded, ctx_div, ctx_hi_s, ctx_lo_s = sem("ctx_loaded"), sem("ctx_div"), sem("ctx_hi_s"), sem("ctx_lo_s")
        codes_in, scales_in = sem("codes_in"), sem("scales_in")
        u_ready, line_ready, pooled = sem("u_ready"), sem("line_ready"), sem("pooled")
        dq_l0, dq_left, dq_code, dq_w = sem("dq_l0"), sem("dq_left"), sem("dq_code"), sem("dq_w")
        gu_hi_s, gu_lo_s = sem("gu_hi_s"), sem("gu_lo_s")
        attn_out, ln_y, ln_st, ln_ag, ln_sd, ln_rs, ln_x = [sem(n) for n in (
            "attn_out", "ln_y", "ln_st", "ln_ag", "ln_sd", "ln_rs", "ln_x")]
        x1T_ps, x1T_hi_s, x1T_lo_s = sem("x1T_ps"), sem("x1T_hi_s"), sem("x1T_lo_s")
        gate_up, silu_s, hid_s = sem("gate_up"), sem("silu_s"), sem("hid_s")
        wd_hi_s, wd_lo_s, hh_s, hl_s, down = sem("wd_hi_s"), sem("wd_lo_s"), sem("hh_s"), sem("hl_s"), sem("down")
        out_s = sem("out_s")

        block = ctx.enter_context(nc.Block())

        K_UNITS = [("k", 0, 0), ("k", 0, 1)] + [("q", mt, hf) for mt in range(KC) for hf in range(NH)]
        NKQ = len(K_UNITS)

        @block.sync
        def _(sp):
            def load_unit(n):
                sp.wait_ge(u_ready, n)
                sp.dma_start(codes[:], t["codes"][bass.ds(n, 1), :, :].rearrange("a p n -> (a p) n")).then_inc(codes_in, 16)
                sp.wait_ge(dq_w, n)
                for b in range(2):
                    sp.dma_start(scales[BLOCK * b:BLOCK * (b + 1), :],
                                 t["scales"][bass.ds(n, 1), b, :].to_broadcast([BLOCK, UNIT])).then_inc(scales_in, 16)

            def load_stack(buf, g):
                for blk, part in enumerate(Q_PART):
                    sp.dma_start(q_stack[buf][HD * blk:HD * (blk + 1), :],
                                 t["q_scr"][part, bass.ds(g * REP * HD, REP * HD), :].rearrange(
                                     "(d r) t -> d (r t)", r=REP)).then_inc(stack_in[buf], 16)
                for blk, part in enumerate(K_PART):
                    sp.dma_start(k_stack[buf][HD * blk:HD * (blk + 1), :],
                                 t["k_scr"][part, bass.ds(g * HD, HD), :]).then_inc(stack_in[buf], 16)

            for kc in range(KC):
                sp.dma_start(xT_raw[:, kc, :], t["xT"][kc * P:(kc + 1) * P, :]).then_inc(xT_in[kc], 16)
                sp.dma_start(w_raw[:, kc, :], t["w_qkv"][kc * P:(kc + 1) * P, :]).then_inc(w_in[kc], 16)
            load_unit_first = t["codes"]
            sp.dma_start(codes[:], load_unit_first[0, :, :]).then_inc(codes_in, 16)
            for b in range(2):
                sp.dma_start(scales[BLOCK * b:BLOCK * (b + 1), :],
                             t["scales"][0:1, b, :].to_broadcast([BLOCK, UNIT])).then_inc(scales_in, 16)
            sp.dma_start(xres[:], t["x"].rearrange("(n p) d -> p n d", p=P)).then_inc(xres_in, 16)
            sp.dma_start(wo_raw[:], t["wo"].rearrange("(c p) n -> p c n", p=P)).then_inc(wo_in, 16)
            sp.dma_start(bo_all[:], t["bo"].rearrange("(a n) -> a n", a=1).to_broadcast([P, D])).then_inc(bo_in, 16)
            for e, (which, mt, hf) in enumerate(K_UNITS):
                sp.wait_ge(parts, e + 1)
                scr = t["k_scr"] if which == "k" else t["q_scr"]
                sp.dma_start(scr[:, mt * P:(mt + 1) * P, hf * HALF:(hf + 1) * HALF].rearrange("c p t -> p c t"),
                             qk_parts[:, 0, :, :]).then_inc(parts_stored, 16)
                if 1 <= e <= EARLY_UNITS - 1:
                    load_unit(e)
            sp.wait_ge(parts_stored, 16 * NKQ)
            sp.wait_ge(x_lo_s, KC)
            sp.wait_ge(w_lo_s, KC)
            load_stack(0, 0)
            load_stack(1, 1)

            def mrows(buf, g):
                sp.wait_ge(nm_all, g + 1)
                for c in range(3):
                    sp.dma_start(q_stack[buf][MROW + c:MROW + c + 1, :].rearrange("a (n q) -> a n q", q=P),
                                 neg_max[:, c, :]).then_inc(mrow_in, 16)

            def group(g, c, last=False, stack=True):
                if stack:
                    sp.wait_ge(st_ready, NST * g + 1)
                    load_stack((c + 2) % 3, g + 2)
                load_unit(g + EARLY_UNITS)
                for hf in range(NH):
                    if hf == 1 and not last:
                        mrows((c + 1) % 3, g + 1)
                    sp.wait_ge(ctx_evac, NH * g + hf + 2)
                    sp.dma_start(t["ctx_scr"][bass.ds(g, 1), :, hf * HALF:(hf + 1) * HALF].rearrange("a p n -> (a p) n"),
                                 ctx_raw[:, hf, :]).then_inc(ctx_stored[hf], 16)

            mrows(0, 0)
            with sp.Fori(0, 2) as it:
                for c in range(3):
                    group(it * 3 + c, c)
            group(6, 0, stack=False)

            def load_ctx(ch):
                for hf in range(NH):
                    sp.wait_ge(ctx_stored[hf], 16 * (2 * (ch + 1) + 1))
                if ch > 0:
                    sp.wait_ge(ctx_lo_s, ch)
                scr = t["ctx_scr"].rearrange("g (r two d) n -> (g r) two d n", two=2, d=HD)
                for k, dst in enumerate((ctx_in, sum_in)):
                    sp.dma_start(dst[:], scr[2 * REP * ch:2 * REP * (ch + 1), k, :, :]).then_inc(ctx_loaded, 16)

            load_ctx(0)
            group(7, 1, last=True, stack=False)
            for ch in range(1, KC):
                load_ctx(ch)
            load_unit(MT)
            load_unit(MT + 1)
            with sp.Fori(1, MT) as j:
                load_unit(MT + 2 * j)
                load_unit(MT + 2 * j + 1)
            for tt in range(TT):
                sp.wait_ge(ln_x, TT + tt + 1)
                sp.dma_start(t["out"][tt * P:(tt + 1) * P, :], xres[:, tt, :]).then_inc(out_s, 16)
            sp.wait_ge(out_s, 16 * TT)

        @block.gpsimd
        def _(pool):
            pool.memset(ident_f[:], 0.0).then_inc(consts, 1)
            pool.memset(ident_b[:], 0.0).then_inc(consts, 1)
            pool.memset(mask_q[:], 0.0).then_inc(consts, 1)
            pool.memset(mask_k[:], 0.0).then_inc(consts, 1)
            pool.memset(eps[:], EPS).then_inc(consts, 1)
            for b in range(3):
                pool.memset(v_ones[b][:, :, HD:32], 1.0).then_inc(consts, 1)
            pool.wait_ge(consts, 4)
            pool.affine_select(out=ident_f[:], in_=ident_f[:], compare_op=ALU.not_equal, fill=1.0, base=0,
                               pattern=[[-1, P]], channel_multiplier=1).then_inc(consts, 1)
            pool.affine_select(out=ident_b[:], in_=ident_b[:], compare_op=ALU.not_equal, fill=1.0, base=0,
                               pattern=[[-1, P]], channel_multiplier=1).then_inc(consts, 1)
            pool.affine_select(out=mask_q[:], in_=mask_q[:], compare_op=ALU.is_ge, fill=NEG, base=0,
                               pattern=[[-1, P]], channel_multiplier=1).then_inc(consts, 1)
            pool.affine_select(out=mask_k[:], in_=mask_k[:], compare_op=ALU.is_ge, fill=NEG, base=0,
                               pattern=[[1, P]], channel_multiplier=-1).then_inc(consts, 1)
            N_CONSTS = 12

            def down_slot(n):
                return w_down[:, bass.ds(n, 1), :].rearrange("p a n -> p (a n)")

            def unit(n, buf, out):
                L = lines[buf]
                for k, src in enumerate((R1, R2, R3)):
                    pool.wait_ge(line_ready, n * NLINE + k + 2)
                    if k:
                        pool.wait_ge(pooled, n * 3 + k)
                    pool.tensor_tensor(L[:, R0, :], L[:, R0, :], L[:, src, :], ALU.add).then_inc(pooled, 1)
                pool.wait_ge(dq_code, n + 1)
                pool.wait_ge(scales_in, 32 * (n + 1))
                pool.tensor_tensor(out, L[:, L0, :], scales[:], ALU.mult).then_inc(dq_w, 1)

            def stage_v(buf, g):
                pool.wait_ge(consts, N_CONSTS)
                pool.tensor_copy(v_ones[buf][:, :, 0:HD], v_all[:, :, bass.ds(g * HD, HD)]).then_inc(v_staged, 1)

            for n in range(EARLY_UNITS):
                unit(n, 0, w_down[:, n, :])
            pool.wait_ge(xres_in, 16)
            pool.wait_ge(bo_in, 16)
            pool.tensor_tensor(xres[:], xres[:], bo_all[:].unsqueeze(1).to_broadcast([P, TT, D]), ALU.add).then_inc(bo_added, 1)
            pool.wait_ge(v_ready, 2)
            pool.tensor_copy(v_ones[0][:, :, 0:HD], v_all[:, :, 0:HD]).then_inc(v_staged, 1)
            with pool.Fori(0, 2) as it:
                for c in range(3):
                    g = it * 3 + c
                    pool.wait_ge(pv_done, NPV * g + 1)
                    stage_v((c + 1) % 3, g + 1)
                    unit(g + EARLY_UNITS, 0, down_slot(g + EARLY_UNITS))
            pool.wait_ge(pv_done, NPV * 6 + 1)
            stage_v(1, 7)
            unit(6 + EARLY_UNITS, 0, w_down[:, 6 + EARLY_UNITS, :])
            unit(7 + EARLY_UNITS, 0, w_down[:, 7 + EARLY_UNITS, :])
            unit(MT, 0, lines[0][:, R1, :])
            unit(MT + 1, 1, lines[1][:, R1, :])
            with pool.Fori(1, MT) as j:
                unit(MT + 2 * j, 0, lines[0][:, R1, :])
                unit(MT + 2 * j + 1, 1, lines[1][:, R1, :])

        @block.scalar
        def _(act):
            def line_pass(n, buf, k, prev, prev_gu=None):
                if k == 0:
                    act.wait_ge(u_ready, n + 1)
                    if prev is not None:
                        act.wait_ge(dq_w, prev + 1)
                    if prev_gu is not None:
                        act.wait_ge(gu_lo_s, prev_gu)
                a, b = LINES[k]
                act.activation(lines[buf][:, k, :], us[buf][:], ACT.Relu, bias=b, scale=a).then_inc(line_ready, 1)

            def unit(n, buf, prev, prev_gu=None):
                for k in range(NLINE):
                    line_pass(n, buf, k, prev, prev_gu)

            act.sem_inc(ctx_evac, 1)
            for hf in range(NH):
                act.sem_inc(ctx_stored[hf], 16)
            for kc in range(KC):
                act.wait_ge(xT_in[kc], 16)
                act.activation(xT_hi[:, kc, :], xT_raw[:, kc, :], ACT.Copy).then_inc(x_hi_s, 1)
                act.wait_ge(w_in[kc], 16)
                act.activation(w_hi[:, kc, :], w_raw[:, kc, :], ACT.Copy).then_inc(w_hi_s, 1)
            for e in range(NKQ):
                act.wait_ge(proj, e + 1)
                if e >= 1:
                    act.wait_ge(parts_stored, 16 * e)
                act.activation(qk_parts[:, 0, 0, :], ps[:, e % 8, :], ACT.Copy).then_inc(part_h, 1)
                if 1 <= e <= EARLY_UNITS:
                    unit(e - 1, 0, e - 2 if e >= 2 else None)
            for hf in range(NH):
                act.wait_ge(proj, NKQ + hf + 1)
                act.activation(v_all[:, 4 * hf:4 * hf + 4, :], ps[:, (NKQ + hf) % 8, :], ACT.Copy).then_inc(v_ready, 1)
            act.wait_ge(wo_in, 16)
            act.activation(wo_hi[:], wo_raw[:], ACT.Copy).then_inc(wo_hi_s, 1)

            def evac(g, hf):
                act.wait_ge(pv_done, NPV * g + (4 if hf == 0 else NPV))
                act.wait_ge(ctx_stored[hf], 16 * (g + 1))
                act.activation(ctx_raw[:, hf, :], ps[:, B_CTX, :], ACT.Copy).then_inc(ctx_evac, 1)

            def group(g, first=False):
                for s, (qh, kt, pr) in enumerate(STEPS):
                    n = (qh + 1) * HALF - q_from(qh, kt)
                    act.wait_ge(st_ready, NST * g + s + 1)
                    if s >= 4 or not first:
                        act.wait_ge(pv_done, NPV * g + (s - 4) // 2 + 1)
                    act.activation(probs[:, s % 4, :, 0:n], ps[:, 2 * (s % 2):2 * (s % 2) + 2, 0:n], ACT.Exp,
                                   scale=SCALE).then_inc(exp_done, 1)
                    if s == 9:
                        evac(g, 0)
                    if 2 <= s < 23 and s % 3 == 2:
                        line_pass(g + EARLY_UNITS, 0, (s - 2) // 3, g + EARLY_UNITS - 1)
                evac(g, 1)

            with act.Fori(0, 2) as it:
                for c in range(3):
                    group(it * 3 + c, first=True)
            group(6, first=True)
            group(7, first=True)

            for ch in range(KC):
                act.wait_ge(ctx_div, ch + 1)
                act.activation(ctx_hi[:, ch, :], sum_in[:], ACT.Copy).then_inc(ctx_hi_s, 1)
            unit(MT, 0, MT - 1)
            for tt in range(TT + 2):
                if tt < TT:
                    act.wait_ge(ln_ag, tt + 1)
                    act.activation(ln_std[:, tt % 4, :], ln_mv[:, tt % 4, 1:2], ACT.Sqrt, bias=eps[:]).then_inc(ln_sd, 1)
                if tt >= 2:
                    act.wait_ge(x1T_ps, tt - 1)
                    act.activation(x1T_hi[:, :, (tt - 2) * P:(tt - 1) * P],
                                   ps[:, 4 + tt % 2, :].rearrange("p (c n) -> p c n", c=KC), ACT.Copy).then_inc(x1T_hi_s, 1)
            act.wait_ge(attn_out, TT)
            unit(MT + 1, 1, None)
            unit(MT + 2, 0, MT, 1)

            def silu(j, par):
                act.wait_ge(gate_up, 2 * j + 1)
                act.activation(hid[:, bass.ds(j, 1), :].rearrange("p a n -> p (a n)"), ps[:, 4 * par:4 * par + 2, :].rearrange(
                    "p a n -> p (a n)"), ACT.Silu).then_inc(silu_s, 1)

            def hidden_tile(j, par, first=False, more=True):
                n = MT + 2 * j + 3
                if not first:
                    silu(j - 1, 1 - par)
                unit(n, 1, n - 2, n - MT - 1)
                if more:
                    unit(n + 1, 0, n - 1, n - MT)

            hidden_tile(0, 0, first=True)
            with act.Fori(1, MT - 3, 2) as j:
                hidden_tile(j, 1)
                hidden_tile(j + 1, 0)
            hidden_tile(MT - 3, 1)
            hidden_tile(MT - 2, 0, more=False)
            silu(MT - 2, 0)
            silu(MT - 1, 1)
            act.wait_ge(gu_lo_s, 2 * MT)
            for j in range(MT):
                act.activation(wd_hi[:, j, :], w_down[:, j, :], ACT.Copy).then_inc(wd_hi_s, 1)
            for tt in range(TT + 1):
                if tt < TT:
                    act.wait_ge(hid_s, MT)
                    if tt >= 2:
                        act.wait_ge(down, tt - 1)
                    else:
                        act.wait_ge(gate_up, 2 * MT)
                    act.activation(hid_hi[tt % 2][:], hid[:, :, tt * P:(tt + 1) * P], ACT.Copy).then_inc(hh_s, 1)
                if tt >= 1:
                    act.wait_ge(ln_ag, TT + tt)
                    act.activation(ln_std[:, (tt - 1) % 4, :], ln_mv[:, (tt - 1) % 4, 1:2], ACT.Sqrt, bias=eps[:]).then_inc(ln_sd, 1)

        @block.vector
        def _(dve):
            def make_u(n, buf, prev):
                dve.wait_ge(codes_in, 16 * (n + 1))
                if prev is not None:
                    dve.wait_ge(line_ready, prev * NLINE + NLINE)
                    dve.wait_ge(dq_w, prev + 1)
                    dve.wait_ge(dq_l0, prev + 1)
                dve.tensor_scalar(us[buf][:], codes[:], float(-ZERO_AT), None, ALU.add).then_inc(u_ready, 1)
                dve.wait_ge(u_ready, n + 1)
                dve.tensor_scalar(lines[buf][:, L0, :], us[buf][:], SLOPE_L0, 0.0, ALU.mult, ALU.max).then_inc(dq_l0, 1)

            def finish_unit(n, buf):
                L = lines[buf]
                for k, src in enumerate((L1, L2, L3)):
                    dve.wait_ge(line_ready, n * NLINE + k + 5)
                    if k:
                        dve.wait_ge(dq_left, n * 3 + k)
                    else:
                        dve.wait_ge(dq_l0, n + 1)
                    dve.tensor_tensor(L[:, L0, :], L[:, L0, :], L[:, src, :], ALU.add).then_inc(dq_left, 1)
                dve.wait_ge(dq_left, n * 3 + 3)
                dve.wait_ge(pooled, n * 3 + 3)
                dve.tensor_tensor(L[:, L0, :], L[:, R0, :], L[:, L0, :], ALU.subtract).then_inc(dq_code, 1)

            for b in range(3):
                dve.memset(k_stack[b][MROW:STACKM, :], 1.0).then_inc(k_ones, 1)
            for kc in range(KC):
                dve.wait_ge(x_hi_s, kc + 1)
                dve.tensor_tensor(xT_lo[:, kc, :], xT_raw[:, kc, :], xT_hi[:, kc, :].bitcast(F32), ALU.subtract).then_inc(x_lo_s, 1)
                dve.wait_ge(w_hi_s, kc + 1)
                dve.tensor_tensor(w_lo[:, kc, :], w_raw[:, kc, :], w_hi[:, kc, :].bitcast(F32), ALU.subtract).then_inc(w_lo_s, 1)
            make_u(0, 0, None)
            for e in range(NKQ):
                dve.wait_ge(part_h, e + 1)
                if e >= 1:
                    dve.wait_ge(parts, e)
                dve.tensor_tensor(resid[:], ps[:, e % 8, :], qk_parts[:, 0, 0, :], ALU.subtract).then_inc(part_r, 1)
                dve.wait_ge(part_r, e + 1)
                dve.tensor_copy(qk_parts[:, 0, 1, :], resid[:]).then_inc(part_m, 1)
                dve.wait_ge(part_m, e + 1)
                dve.tensor_tensor(qk_parts[:, 0, 2, :], resid[:], qk_parts[:, 0, 1, :], ALU.subtract).then_inc(parts, 1)
                if 2 <= e <= EARLY_UNITS + 1:
                    finish_unit(e - 2, 0)
                    if e - 1 < EARLY_UNITS:
                        make_u(e - 1, 0, e - 2)
            dve.wait_ge(wo_hi_s, 1)
            dve.tensor_tensor(wo_lo[:], wo_raw[:], wo_hi[:].bitcast(F32), ALU.subtract).then_inc(wo_lo_s, 1)

            def reduce(idx, k, buf):
                i, kh, r = MAX_TILES[k]
                n = width(i, kh)
                dve.wait_ge(max_scores, idx + 1)
                dst = row_max[:, buf, r * TT + i:r * TT + i + 1] if kh == 0 else row_max_hi[:, r, i - 4:i - 3]
                dve.reduce_max(dst, ps[:, B_MAX + k % 2, 0:n], AX.X).then_inc(max_done, 1)

            def combine(g, buf):
                dve.wait_ge(max_done, NMAX * g + NMAX)
                v = row_max[:, buf, :].rearrange("p (r i) -> p r i", r=REP)[:, :, 4:8]
                dve.tensor_tensor(v, v, row_max_hi[:], ALU.max).then_inc(max_all, 1)

            def negate(g, first=False):
                dve.wait_ge(max_T, g + 1)
                if not first:
                    dve.wait_ge(mrow_in, 48 * g)
                tr = ps[0:32, B_TR, 0:P]
                dve.tensor_scalar(neg_max[:, 0, :], tr, -1.0, None, ALU.mult).then_inc(nm_h, 1)
                dve.wait_ge(nm_h, g + 1)
                dve.scalar_tensor_tensor(neg_max_f[:], tr, -1.0, neg_max[:, 0, :], ALU.mult, ALU.subtract).then_inc(nm_r, 1)
                dve.wait_ge(nm_r, g + 1)
                dve.tensor_copy(neg_max[:, 1, :], neg_max_f[:]).then_inc(nm_m, 1)
                dve.wait_ge(nm_m, g + 1)
                dve.tensor_tensor(neg_max[:, 2, :], neg_max_f[:], neg_max[:, 1, :], ALU.subtract).then_inc(nm_all, 1)

            for k in range(NMAX):
                reduce(k, k, 0)
            combine(0, 0)
            negate(0, first=True)
            for k in range(LEAD):
                reduce(NMAX + k, k, 1)

            def group(g, c, count=NMAX):
                n = g + EARLY_UNITS
                make_u(n, 0, n - 1)
                for s in range(count):
                    k = (LEAD + s) % NMAX
                    if s == 0:
                        dve.wait_ge(max_all, g + 1)
                    reduce(NMAX * (g + 1) + LEAD + s, k, (c + 1 + (LEAD + s) // NMAX) % 3)
                    if s == NMAX - LEAD - 1:
                        combine(g + 1, (c + 1) % 3)
                    if s == NMAX - LEAD + 1:
                        negate(g + 1)
                if count == NMAX - LEAD:
                    negate(g + 1)
                finish_unit(n, 0)

            with dve.Fori(0, 2) as it:
                for c in range(3):
                    group(it * 3 + c, c)
            group(6, 0, count=NMAX - LEAD)
            make_u(7 + EARLY_UNITS, 0, 6 + EARLY_UNITS)

            def divide(ch):
                dve.wait_ge(ctx_loaded, 32 * (ch + 1))
                if ch > 0:
                    dve.wait_ge(ctx_lo_s, ch)
                dve.reciprocal(sum_in[:], sum_in[:]).then_inc(ln_rs, 1)
                dve.wait_ge(ln_rs, ch + 1)
                dve.tensor_tensor(sum_in[:], ctx_in[:], sum_in[:], ALU.mult).then_inc(ctx_div, 1)

            def ctx_low(ch):
                dve.wait_ge(ctx_hi_s, ch + 1)
                dve.tensor_tensor(ctx_lo[:, ch, :], sum_in[:], ctx_hi[:, ch, :].bitcast(F32), ALU.subtract).then_inc(ctx_lo_s, 1)

            finish_unit(7 + EARLY_UNITS, 0)
            for ch in range(KC):
                divide(ch)
                ctx_low(ch)
            RS0 = KC

            def ln_front(n, tt, src):
                dve.tensor_tensor(xres[:, tt, :], src, xres[:, tt, :], ALU.add).then_inc(ln_y, 1)
                dve.wait_ge(ln_y, n + 1)
                dve.bn_stats(ln_stats[:, n % 2, :], xres[:, tt, :]).then_inc(ln_st, 1)
                dve.wait_ge(ln_st, n + 1)
                dve.bn_aggr(ln_mv[:, n % 4, :], ln_stats[:, n % 2, :]).then_inc(ln_ag, 1)

            def ln_back(n, tt):
                dve.wait_ge(ln_sd, n + 1)
                dve.reciprocal(ln_rstd[:, n % 4, :], ln_std[:, n % 4, :]).then_inc(ln_rs, 1)
                dve.wait_ge(ln_rs, RS0 + n + 1)
                dve.wait_ge(ln_ag, n + 1)
                dve.tensor_scalar(xres[:, tt, :], xres[:, tt, :], ln_mv[:, n % 4, 0:1], ln_rstd[:, n % 4, :],
                                  ALU.subtract, ALU.mult).then_inc(ln_x, 1)

            make_u(MT, 0, MT - 1)
            dve.wait_ge(bo_added, 1)
            for tt in range(TT + 2):
                if tt < TT:
                    dve.wait_ge(attn_out, tt + 1)
                    ln_front(tt, tt, ps[:, tt % 4, :])
                if 1 <= tt <= TT:
                    ln_back(tt - 1, tt - 1)
                if tt >= 2:
                    dve.wait_ge(x1T_hi_s, tt - 1)
                    dve.tensor_tensor(x1T_lo[:, :, (tt - 2) * P:(tt - 1) * P],
                                      ps[:, 4 + tt % 2, :].rearrange("p (c n) -> p c n", c=KC),
                                      x1T_hi[:, :, (tt - 2) * P:(tt - 1) * P].bitcast(F32), ALU.subtract).then_inc(x1T_lo_s, 1)
            def split_gu(n, par, which):
                w = lines[which][:, R1, :]
                dve.wait_ge(dq_w, n + 1)
                dve.tensor_copy(gu_hi[:, par, which, :], w).then_inc(gu_hi_s, 1)
                dve.wait_ge(gu_hi_s, n - MT + 1)
                dve.tensor_tensor(gu_lo[:, par, which, :], w, gu_hi[:, par, which, :].bitcast(F32),
                                  ALU.subtract).then_inc(gu_lo_s, 1)

            finish_unit(MT, 0)
            split_gu(MT, 0, 0)
            dve.wait_ge(attn_out, TT)
            make_u(MT + 1, 1, None)
            make_u(MT + 2, 0, MT)
            finish_unit(MT + 1, 1)
            split_gu(MT + 1, 0, 1)
            make_u(MT + 3, 1, MT + 1)

            def hidden_product(j, par):
                dve.wait_ge(gate_up, 2 * j + 2)
                dve.wait_ge(silu_s, j + 1)
                slot = hid[:, bass.ds(j, 1), :].rearrange("p a n -> p (a n)")
                dve.tensor_tensor(slot, slot, ps[:, 4 * par + 2:4 * par + 4, :].rearrange("p a n -> p (a n)"),
                                  ALU.mult).then_inc(hid_s, 1)

            def hidden_tile(j, par, first=False, more=True):
                n = MT + 2 * j + 2
                finish_unit(n, 0)
                if not first:
                    hidden_product(j - 1, 1 - par)
                split_gu(n, 1 - par, 0)
                if more:
                    make_u(n + 2, 0, n)
                finish_unit(n + 1, 1)
                split_gu(n + 1, 1 - par, 1)
                if more:
                    make_u(n + 3, 1, n + 1)

            hidden_tile(0, 0, first=True)
            with dve.Fori(1, MT - 3, 2) as j:
                hidden_tile(j, 1)
                hidden_tile(j + 1, 0)
            hidden_tile(MT - 3, 1)
            hidden_tile(MT - 2, 0, more=False)
            hidden_product(MT - 2, 0)
            hidden_product(MT - 1, 1)

            for tt in range(TT + 1):
                if tt < TT:
                    dve.wait_ge(hh_s, tt + 1)
                    dve.tensor_tensor(hid_lo[tt % 2][:], hid[:, :, tt * P:(tt + 1) * P], hid_hi[tt % 2][:].bitcast(F32),
                                      ALU.subtract).then_inc(hl_s, 1)
                if tt == 0:
                    for j in range(MT):
                        dve.wait_ge(wd_hi_s, j + 1)
                        dve.tensor_tensor(wd_lo[:, j, :], w_down[:, j, :], wd_hi[:, j, :].bitcast(F32),
                                          ALU.subtract).then_inc(wd_lo_s, 1)
                if tt >= 1:
                    dve.wait_ge(down, tt)
                    ln_front(TT + tt - 1, tt - 1, ps[:, (tt - 1) % 2, :])
                    ln_back(TT + tt - 1, tt - 1)

        @block.tensor
        def _(pe):
            def three_pass(out, a_hi, a_lo, b_hi, b_lo, chunks):
                mm, n = None, 3 * len(chunks)
                at_ = 0
                for c in chunks:
                    for a, b in ((a_hi, b_hi), (a_hi, b_lo), (a_lo, b_hi)):
                        mm = pe.matmul(out, a(c), b(c), start=at_ == 0, stop=at_ == n - 1)
                        at_ += 1
                return mm

            for kc in range(KC):
                pe.wait_ge(x_lo_s, kc + 1)
                pe.wait_ge(w_lo_s, kc + 1)
            for e, (which, mt, hf) in enumerate(K_UNITS):
                col = (4 * P if which == "k" else mt * P)
                if e >= 8:
                    pe.wait_ge(parts, e - 7)
                three_pass(ps[:, e % 8, :], lambda c: w_hi[:, c, col:col + P], lambda c: w_lo[:, c, col:col + P],
                           lambda c: xT_hi[:, c, hf * HALF:(hf + 1) * HALF],
                           lambda c: xT_lo[:, c, hf * HALF:(hf + 1) * HALF], range(KC)).then_inc(proj, 1)
            for hf in range(NH):
                bank = (NKQ + hf) % 8
                pe.wait_ge(parts, NKQ + hf - 7)
                for q4 in range(4):
                    tok = (4 * hf + q4) * P
                    mm = three_pass(ps[:, bank, q4 * P:(q4 + 1) * P], lambda c: xT_hi[:, c, tok:tok + P],
                                    lambda c: xT_lo[:, c, tok:tok + P], lambda c: w_hi[:, c, 5 * P:6 * P],
                                    lambda c: w_lo[:, c, 5 * P:6 * P], range(KC))
                mm.then_inc(proj, 1)

            def max_tile(idx, k, buf, free):
                i, kh, r = MAX_TILES[k]
                n = width(i, kh)
                bank = B_MAX + k % 2
                diag = n < HALF or (i + 1) * P == (kh + 1) * HALF
                if free:
                    pe.wait_ge(max_done, idx - 1)
                mm = pe.matmul(ps[:, bank, 0:n], q_stack[buf][0:STACK, r * T + i * P:r * T + (i + 1) * P],
                               k_stack[buf][0:STACK, kh * HALF:kh * HALF + n], start=True, stop=not diag)
                if diag:
                    mm = pe.matmul(ps[:, bank, n - P:n], ident_b[:], mask_q[:], start=False, stop=True)
                mm.then_inc(max_scores, 1)

            def transpose_max(g, buf, first=False):
                pe.wait_ge(max_all, g + 1)
                if not first:
                    pe.wait_ge(nm_all, g)
                pe.transpose(ps[0:32, B_TR, 0:P], row_max[:, buf, :], ident_f[:]).then_inc(max_T, 1)

            def score_step(g, s, buf, first):
                qh, kt, pr = STEPS[s]
                q0 = q_from(qh, kt)
                n = (qh + 1) * HALF - q0
                diag = q0 == kt * P
                if s >= 2 or not first:
                    pe.wait_ge(exp_done, NST * g + s - 1)
                for a in range(2):
                    r = 2 * pr + a
                    bank = 2 * (s % 2) + a
                    mm = pe.matmul(ps[:, bank, 0:n], k_stack[buf][0:STACKM, kt * P:(kt + 1) * P],
                                   q_stack[buf][0:STACKM, r * T + q0:r * T + q0 + n], start=True, stop=not diag)
                    if diag:
                        mm = pe.matmul(ps[:, bank, 0:P], ident_b[:], mask_k[:], start=False, stop=True)
                mm.then_inc(st_ready, 1)

            def pv(g, m, buf):
                qh, kt, _ = STEPS[2 * m]
                off = q_from(qh, kt) - qh * HALF
                n = HALF - off
                pe.wait_ge(exp_done, NST * g + 2 * m + 2)
                if m == 0:
                    pe.wait_ge(ctx_evac, NH * g + 1)
                if m == 4:
                    pe.wait_ge(ctx_evac, NH * g + 2)
                for r in range(REP):
                    s = 2 * m + r // 2
                    mm = pe.matmul(ps[32 * r:32 * r + 32, B_CTX, off:HALF], v_ones[buf][:, kt, :],
                                   probs[:, s % 4, r % 2, 0:n], start=kt == 0, stop=kt == 4 * (qh + 1) - 1)
                mm.then_inc(pv_done, 1)

            pe.wait_ge(consts, 12)
            pe.wait_ge(k_ones, 3)
            pe.wait_ge(stack_in[0], 192)
            pe.wait_ge(part_h, NKQ)
            pe.wait_ge(v_ready, 2)
            for k in range(NMAX):
                max_tile(k, k, 0, free=k >= 2)
            pe.wait_ge(stack_in[1], 192)
            for k in range(LEAD):
                max_tile(NMAX + k, k, 1, free=True)
                if k == 1:
                    transpose_max(0, 0, first=True)

            def group(g, it, c, count=NMAX):
                pe.wait_ge(mrow_in, 48 * (g + 1))
                pe.wait_ge(v_staged, g + 1)
                for s in range(NST):
                    score_step(g, s, c, first=True)
                    for k in (2 * s, 2 * s + 1):
                        if k >= count:
                            continue
                        kk = (LEAD + k) % NMAX
                        if k == NMAX - LEAD:
                            pe.wait_ge(stack_in[(c + 2) % 3], 192 * (it + (c + 2) // 3 + 1))
                        max_tile(NMAX * (g + 1) + LEAD + k, kk, (c + 1 + (LEAD + k) // NMAX) % 3, free=True)
                        if k == NMAX - LEAD + 1 or (k == count - 1 and count == NMAX - LEAD):
                            transpose_max(g + 1, (c + 1) % 3)
                    if s >= 2 and s % 2 == 0:
                        pv(g, s // 2 - 1, c)
                pv(g, NPV - 1, c)

            with pe.Fori(0, 2) as it:
                for c in range(3):
                    group(it * 3 + c, it, c)
            group(6, 2, 0, count=NMAX - LEAD)
            group(7, 2, 1, count=0)

            pe.wait_ge(wo_lo_s, 1)

            def wo_tile(tt):
                if tt >= 4:
                    pe.wait_ge(ln_y, tt - 3)
                three_pass(ps[:, tt % 4, :], lambda c: ctx_hi[:, c, tt * P:(tt + 1) * P],
                           lambda c: ctx_lo[:, c, tt * P:(tt + 1) * P], lambda c: wo_hi[:, c, :],
                           lambda c: wo_lo[:, c, :], range(KC)).then_inc(attn_out, 1)

            def x1_transpose(tt):
                pe.wait_ge(ln_x, tt + 1)
                if tt >= 2:
                    pe.wait_ge(x1T_lo_s, tt - 1)
                for c in range(KC):
                    mm = pe.transpose(ps[:, 4 + tt % 2, c * P:(c + 1) * P], xres[:, tt, c * P:(c + 1) * P], ident_f[:])
                mm.then_inc(x1T_ps, 1)

            pe.wait_ge(exp_done, NST * G)
            pe.wait_ge(ctx_lo_s, KC)
            for tt in range(TT + 1):
                if tt < TT:
                    wo_tile(tt)
                if tt >= 1:
                    x1_transpose(tt - 1)

            def hidden_tile(j, par, first=False):
                if first:
                    pe.wait_ge(x1T_lo_s, TT)
                    pe.wait_ge(ln_y, TT)
                else:
                    pe.wait_ge(hid_s, j - 1)
                for which in range(2):
                    pe.wait_ge(gu_lo_s, 2 * j + which + 1)
                    for hf in range(NH):
                        mm = three_pass(ps[:, 4 * par + 2 * which + hf, :],
                                        lambda c: gu_hi[:, par, which, c * P:(c + 1) * P],
                                        lambda c: gu_lo[:, par, which, c * P:(c + 1) * P],
                                        lambda c: x1T_hi[:, c, hf * HALF:(hf + 1) * HALF],
                                        lambda c: x1T_lo[:, c, hf * HALF:(hf + 1) * HALF], range(KC))
                    mm.then_inc(gate_up, 1)

            hidden_tile(0, 0, first=True)
            hidden_tile(1, 1, first=True)
            with pe.Fori(2, MT, 2) as j:
                hidden_tile(j, 0)
                hidden_tile(j + 1, 1)

            for tt in range(TT):
                pe.wait_ge(hl_s, tt + 1)
                if tt >= 2:
                    pe.wait_ge(ln_y, TT + tt - 1)
                else:
                    pe.wait_ge(hid_s, MT)
                for j in range(MT):
                    if tt == 0:
                        pe.wait_ge(wd_lo_s, j + 1)
                    for p3, (a, b) in enumerate(((hid_hi, wd_hi), (hid_hi, wd_lo), (hid_lo, wd_hi))):
                        mm = pe.matmul(ps[:, tt % 2, :], a[tt % 2][:, j, :], b[:, j, :],
                                       start=j == 0 and p3 == 0, stop=j == MT - 1 and p3 == 2)
                mm.then_inc(down, 1)


def kernel(L0_attn_x, L0_attn_Wq, L0_attn_Wkv, L0_attn_Wo, L0_attn_bo, L0_ffn_gate_q, L0_ffn_gate_absmax,
           L0_ffn_up_q, L0_ffn_up_absmax, L0_ffn_down_q, L0_ffn_down_absmax):
    import concourse.bacc as bacc
    from concourse.bass_utils import run_bass_kernel_spmd

    x = np.asarray(L0_attn_x)[0]
    wq = np.asarray(L0_attn_Wq).reshape(D, G, REP, HD).transpose(0, 1, 3, 2).reshape(D, D)
    wkv = np.asarray(L0_attn_Wkv).reshape(D, G, 2, HD).transpose(0, 2, 1, 3).reshape(D, 2 * G * HD)

    def wide(q):
        return np.asarray(q).reshape(MT, P, KC, P).transpose(0, 3, 2, 1).reshape(MT, P, UNIT)

    def wide_scale(a):
        return np.asarray(a).reshape(MT, P, KC, 2).transpose(0, 3, 2, 1).reshape(MT, 2, UNIT)

    gate_up = np.stack([wide(L0_ffn_gate_q), wide(L0_ffn_up_q)], 1).reshape(2 * MT, P, UNIT)
    gate_up_s = np.stack([wide_scale(L0_ffn_gate_absmax), wide_scale(L0_ffn_up_absmax)], 1).reshape(2 * MT, 2, UNIT)
    down = np.asarray(L0_ffn_down_q).T.reshape(MT, P, UNIT)
    down_s = np.asarray(L0_ffn_down_absmax).reshape(D, 2 * MT).T.reshape(MT, 2, UNIT)
    arrays = {
        "x": x, "xT": x.T, "w_qkv": np.concatenate([wq, wkv], 1), "wo": np.asarray(L0_attn_Wo),
        "bo": np.asarray(L0_attn_bo),
        "codes": np.concatenate([down, gate_up], 0), "scales": np.concatenate([down_s, gate_up_s], 0),
    }
    arrays = {k: np.ascontiguousarray(v) for k, v in arrays.items()}
    nc = bacc.Bacc("TRN2", target_bir_lowering=False, num_devices=1)
    t = {k: nc.dram_tensor(k, list(v.shape), mybir.dt.from_np(v.dtype), kind="ExternalInput").ap()
         for k, v in arrays.items()}
    t["q_scr"] = nc.dram_tensor("q_scr", [3, D, T], BF16, kind="Internal").ap()
    t["k_scr"] = nc.dram_tensor("k_scr", [3, P, T], BF16, kind="Internal").ap()
    t["ctx_scr"] = nc.dram_tensor("ctx_scr", [G, P, T], F32, kind="Internal").ap()
    t["out"] = nc.dram_tensor("out", [T, D], F32, kind="ExternalOutput").ap()
    build_program(nc, t)
    r = run_bass_kernel_spmd(nc, [arrays], core_ids=[0])
    return np.asarray(r.results[0]["out"]).reshape(1, T, D)
```

```python
from contextlib import ExitStack

import numpy as np

import concourse.bass as bass
import concourse.mybir as mybir

F32, F32R, BF16, I32 = mybir.dt.float32, mybir.dt.float32r, mybir.dt.bfloat16, mybir.dt.int32
ALU, ACT, AX = mybir.AluOpType, mybir.ActivationFunctionType, mybir.AxisListType

P = 128
T, D, H, G = 1024, 512, 32, 8
HD = D // H
REP = H // G
KC = D // P
TT = T // P
HALF, NH = 512, T // 512
M = 1792
MT = M // P
BLOCK = 64
UNIT = 512
UNITS = 3 * MT
EPS = 1e-5
NEG = -3.0e38
SCALE = 1.0 / HD ** 0.5

Q_PART = (0, 0, 0, 1, 1, 2)
K_PART = (0, 1, 2, 0, 1, 0)
STACK = HD * len(Q_PART)
MROW = STACK
STACKM = STACK + 3

CODE = np.array([-1.0, -0.6961928009986877, -0.5250730514526367, -0.39491748809814453,
                 -0.28444138169288635, -0.18477343022823334, -0.09105003625154495, 0.0,
                 0.07958029955625534, 0.16093020141124725, 0.24611230194568634, 0.33791524171829224,
                 0.44070982933044434, 0.5626170039176941, 0.7229568362236023, 1.0], np.float32)
ZERO_AT = 7


def hinges(side, starts):
    def fma(a, u, b):
        return np.float32(np.float64(a) * u + np.float64(b))

    def ulps(v, n):
        return (np.array([v], np.float32).view(np.int32) + np.int32(n)).view(np.float32)[0]

    want = {v: side * CODE[ZERO_AT + side * v] for v in range(1 + (8 if side > 0 else 7))}
    total, terms = {v: np.float32(0) for v in want}, []

    def search(v0):
        pts = [v for v in (v0, v0 + 1) if v in want]
        rest = [np.float64(want[v]) - np.float64(total[v]) for v in pts]
        slope = np.float32(rest[1] - rest[0] if len(pts) == 2 else 2 * rest[0])
        for da in sorted(range(-400, 401), key=abs):
            a = ulps(slope, da)
            for db in range(-3, 4):
                b = ulps(np.float32(rest[0] - np.float64(a) * v0), db) if v0 else np.float32(0)
                if (all(total[v] + max(fma(a, v, b), np.float32(0)) == want[v] for v in pts)
                        and all(fma(a, v, b) <= 0 for v in range(-8, v0))):
                    return a, b
        raise ValueError(v0)

    for v0 in starts:
        a, b = search(v0)
        terms.append((float(side * a), float(b)))
        for v in want:
            total[v] = total[v] + max(fma(a, v, b), np.float32(0))
    return terms


RIGHT, LEFT = hinges(1, (1, 3, 5, 7)), hinges(-1, (0, 2, 4, 6))
R0, R1, R2, R3, L1, L2, L3, L0 = range(8)
NLINE = 7
LINES = RIGHT + LEFT[1:]
SLOPE_L0 = LEFT[0][0]

LEAD = 8
MAX_TILES = [(i, kh, r) for i, kh in [(1, 0), (0, 0), (3, 0), (2, 0), (5, 1), (4, 1), (4, 0), (5, 0), (6, 0),
                                      (7, 0), (7, 1), (6, 1)] for r in range(REP)]
NMAX = len(MAX_TILES)
STEPS = [(qh, kt, pr) for qh in range(NH) for kt in range(4 * (qh + 1)) for pr in range(2)]
NST = len(STEPS)
NPV = NST // 2

EARLY_UNITS = 4
LOOP_UNITS = (2, 2, 1)
ATTN_UNITS = EARLY_UNITS + 2 * sum(LOOP_UNITS) + 4
NW = (UNITS - ATTN_UNITS) // 2
FREE = 1


def width(i, kh):
    return min(HALF, (i + 1) * P - kh * HALF)


def q_from(qh, kt):
    return max(qh * HALF, kt * P)


def build_program(nc, t):
    ctx = ExitStack()
    with ctx:
        base = (nc.sbuf_base + 63) // 64 * 64

        def at(name, kib, shape, dt):
            return nc.alloc_sbuf_tensor_at(name, shape, dt, offset=base + int(kib * 1024))

        xres = at("xres", 0, [P, TT, D], F32)
        ident_f = at("ident_f", 16, [P, P], F32)
        ident_b = at("ident_b", 16.5, [P, P], BF16)
        mask_q = at("mask_q", 16.75, [P, P], BF16)
        mask_k = at("mask_k", 17, [P, P], BF16)
        row_max = at("row_max", 17.25, [P, 3, 32], F32)
        row_max_hi = at("row_max_hi", 17.625, [P, REP, 4], F32)
        eps = at("eps", 17.6875, [P, 1], F32)
        ln_stats = at("ln_stats", 17.71875, [P, 2, 6], F32)
        ln_mv = at("ln_mv", 17.78125, [P, 4, 2], F32)
        ln_std = at("ln_std", 17.8125, [P, 4, 1], F32)
        ln_rstd = at("ln_rstd", 17.84375, [P, 4, 1], F32)
        ln_nb = at("ln_nb", 17.875, [P, 4, 1], F32)
        w_down = at("w_down", 18, [P, MT, UNIT], F32)
        codes = [at("codes_a", 46, [P, UNIT], I32), at("codes_b", 67, [P, UNIT], I32)]
        scales = [at("scales_a", 48, [P, UNIT], F32), at("scales_b", 69, [P, UNIT], F32)]
        wo_hi = at("wo_hi", 67, [P, KC, D], F32R)
        wo_lo = at("wo_lo", 75, [P, KC, D], F32R)
        xT_raw = at("xT_raw", 83, [P, KC, T], F32)
        w_raw = at("w_raw", 99, [P, KC, 6 * P], F32)
        q_stack = [at(f"q_stack{b}", 83 + 8 * b, [P, REP * T], BF16) for b in range(3)]
        x1T_hi = at("x1T_hi", 83, [P, KC, T], F32R)
        x1T_lo = at("x1T_lo", 99, [P, KC, T], F32R)
        E = 115
        us = [at("u_a", 50, [P, UNIT], BF16), at("u_b", E + 88, [P, UNIT], BF16)]
        lines = [at("lines_a", 51, [P, 8, UNIT], F32), at("lines_b", E + 72, [P, 8, UNIT], F32)]
        w_hi = at("w_hi", E, [P, KC, 6 * P], F32R)
        w_lo = at("w_lo", E + 12, [P, KC, 6 * P], F32R)
        probs = at("probs", E, [P, 4, 2, HALF], F32)
        wo_raw = at("wo_raw", E + 16, [P, KC, D], F32)
        ctx_raw = at("ctx_raw", E + 24, [P, NH, HALF], F32)
        ctx_in = at("ctx_in", E + 28, [P, T], F32)
        rsum_in = at("rsum_in", E + 32, [P, T], F32)
        qk_parts = at("qk_parts", E + 28, [P, 2, 3, HALF], BF16)
        resid = at("resid", E + 34, [P, HALF], F32)
        v_all = at("v_all", E + 36, [P, TT, P], F32)
        v_ones = [at(f"v_ones{b}", E + 40 + b, [P, TT, 32], F32) for b in range(3)]
        k_stack = [at(f"k_stack{b}", E + 43 + 2 * b, [P, T], BF16) for b in range(3)]
        neg_max = at("neg_max", E + 49, [32, 3, P], BF16)
        neg_max_f = at("neg_max_f", E + 49.75, [32, P], F32)
        sums = at("sums", E + 50.25, [P, T // HD], F32)
        xT_hi = at("xT_hi", E + 56, [P, KC, T], F32R)
        xT_lo = at("xT_lo", E + 72, [P, KC, T], F32R)
        ctx_hi = at("ctx_hi", E + 56, [P, KC, T], F32R)
        ctx_lo = at("ctx_lo", E + 72, [P, KC, T], F32R)
        bo_all = at("bo_all", 204, [P, D], F32)
        gu_hi = at("gu_hi", E, [P, 2, 2 * UNIT], F32R)
        gu_lo = at("gu_lo", E + 8, [P, 2, 2 * UNIT], F32R)
        hid = at("hid", E + 16, [P, MT, T], F32)
        wd_hi = at("wd_hi", 46, [P, MT, D], F32R)
        wd_lo = at("wd_lo", 83, [P, MT, D], F32R)
        hid_hi = [at("hid_hi0", E, [P, MT, P], F32R), at("hid_hi1", E + 72, [P, MT, P], F32R)]
        hid_lo = [at("hid_lo0", E + 7, [P, MT, P], F32R), at("hid_lo1", E + 79, [P, MT, P], F32R)]

        ps = nc.alloc_psum_tensor("ps", [P, 8, HALF], F32)
        B_MAX, B_CTX, B_TR = 4, 6, 7

        def sem(name):
            return ctx.enter_context(nc.semaphore(name))

        def sems(*names):
            return [sem(n) for n in names]

        xT_in = [sem(f"xT_in{k}") for k in range(KC)]
        w_in = [sem(f"w_in{k}") for k in range(KC)]
        xres_in, bo_in, wo_in, consts, k_ones = sems("xres_in", "bo_in", "wo_in", "consts", "k_ones")
        x_hi_s, x_lo_s, w_hi_s, w_lo_s, wo_hi_s, wo_lo_s = sems("x_hi_s", "x_lo_s", "w_hi_s", "w_lo_s", "wo_hi_s", "wo_lo_s")
        bo_added, proj, v_proj, v_ready, v_staged = sems("bo_added", "proj", "v_proj", "v_ready", "v_staged")
        part_h, part_r, part_m, parts = sems("part_h", "part_r", "part_m", "parts")
        parts_stored = [sem(f"parts_stored{b}") for b in range(2)]
        stack_in = [sem(f"stack_in{b}") for b in range(3)]
        max_scores, max_done, max_all, max_T = sems("max_scores", "max_done", "max_all", "max_T")
        nm_h, nm_r, nm_m, nm_all, mrow_in = sems("nm_h", "nm_r", "nm_m", "nm_all", "mrow_in")
        st_ready, exp_done, pv_done, ctx_evac = sems("st_ready", "exp_done", "pv_done", "ctx_evac")
        ctx_stored = [sem(f"ctx_stored{h}") for h in range(NH)]
        sums_in, sums_inv, rsum_stored, rsum_loaded, ctx_loaded = sems("sums_in", "sums_inv", "rsum_stored", "rsum_loaded", "ctx_loaded")
        ctx_mul, ctx_hi_s, ctx_lo_s = sems("ctx_mul", "ctx_hi_s", "ctx_lo_s")
        codes_in = [sem(f"codes_in{b}") for b in range(2)]
        scales_in = [sem(f"scales_in{b}") for b in range(2)]
        u_ready, line_ready, right_sum, left_pool, left_dve = sems("u_ready", "line_ready", "right_sum", "left_pool", "left_dve")
        dq_l0, dq_code, dq_w = sems("dq_l0", "dq_code", "dq_w")
        gu_hi_s, gu_lo_s = sems("gu_hi_s", "gu_lo_s")
        attn_out, ln_y, ln_st, ln_ag, ln_sd, ln_rs, ln_b, ln_x = sems(
            "attn_out", "ln_y", "ln_st", "ln_ag", "ln_sd", "ln_rs", "ln_b", "ln_x")
        x1T_ps, x1T_hi_s, x1T_lo_s = sems("x1T_ps", "x1T_hi_s", "x1T_lo_s")
        gate_up, silu_s, hid_s = sems("gate_up", "silu_s", "hid_s")
        wd_hi_s, wd_lo_s, hh_s, hl_s, down, out_s = sems("wd_hi_s", "wd_lo_s", "hh_s", "hl_s", "down", "out_s")

        block = ctx.enter_context(nc.Block())

        KQ = [("k", 0, 0), ("k", 0, 1)] + [("q", mt, hf) for mt in range(KC) for hf in range(NH)]
        NKQ = len(KQ)
        EARLY_MAX = 6

        def unit_slot(n):
            if isinstance(n, int) and n >= MT:
                return hid[:, (n - MT) // 2, (n - MT) % 2 * UNIT:((n - MT) % 2 + 1) * UNIT]
            return w_down[:, bass.ds(n, 1), :].rearrange("p a n -> p (a n)")

        def window_slot(j, which):
            return hid[:, bass.ds(j + (ATTN_UNITS - MT) // 2, 1), which * UNIT:(which + 1) * UNIT].rearrange(
                "p a n -> p (a n)")

        @block.sync
        def _(sp):
            def load_stack(buf, g):
                for blk, part in enumerate(Q_PART):
                    sp.dma_start(q_stack[buf][HD * blk:HD * (blk + 1), :],
                                 t["q_scr"][part, bass.ds(g * REP * HD, REP * HD), :].rearrange(
                                     "(d r) t -> d (r t)", r=REP)).then_inc(stack_in[buf], 16)
                for blk, part in enumerate(K_PART):
                    sp.dma_start(k_stack[buf][HD * blk:HD * (blk + 1), :],
                                 t["k_scr"][part, bass.ds(g * HD, HD), :]).then_inc(stack_in[buf], 16)

            def mrows(buf, g):
                sp.wait_ge(nm_all, g + 1)
                for c in range(3):
                    sp.dma_start(q_stack[buf][MROW + c:MROW + c + 1, :].rearrange("a (n q) -> a n q", q=P),
                                 neg_max[:, c, :]).then_inc(mrow_in, 16)

            def store_ctx(g, hf):
                sp.wait_ge(ctx_evac, NH * g + hf + 1 + FREE)
                sp.dma_start(t["ctx_scr"][bass.ds(g, 1), :, hf * HALF:(hf + 1) * HALF].rearrange("a p n -> (a p) n"),
                             ctx_raw[:, hf, :]).then_inc(ctx_stored[hf], 16)

            scr = t["ctx_scr"].rearrange("g (r two d) n -> (g r) two d n", two=2, d=HD)

            def load_ctx(ch):
                for hf in range(NH):
                    sp.wait_ge(ctx_stored[hf], 16 * (2 * (ch + 1) + FREE))
                heads = slice(2 * REP * ch, 2 * REP * (ch + 1))
                if ch:
                    sp.wait_ge(rsum_stored, 16 * ch)
                sp.dma_start(sums[:], scr[heads, 1, 0, :].rearrange("h (a b) -> h a b", a=HD)).then_inc(sums_in, 16)
                if ch:
                    sp.wait_ge(ctx_mul, ch)
                sp.dma_start(ctx_in[:], scr[heads, 0, :, :]).then_inc(ctx_loaded, 16)
                sp.wait_ge(sums_inv, ch + 1)
                sp.dma_start(t["rsum_scr"][ch, :, :].rearrange("h (a b) -> h a b", a=HD), sums[:]).then_inc(rsum_stored, 16)
                sp.wait_ge(rsum_stored, 16 * (ch + 1))
                if ch:
                    sp.wait_ge(ctx_lo_s, ch)
                sp.dma_start(rsum_in[:], t["rsum_scr"][ch, :, :].unsqueeze(1).to_broadcast([2 * REP, HD, T])).then_inc(rsum_loaded, 16)

            for kc in range(KC):
                sp.dma_start(xT_raw[:, kc, :], t["xT"][kc * P:(kc + 1) * P, :]).then_inc(xT_in[kc], 16)
                sp.dma_start(w_raw[:, kc, :], t["w_qkv"][kc * P:(kc + 1) * P, :]).then_inc(w_in[kc], 16)
            for e, (which, mt, hf) in enumerate(KQ):
                sp.wait_ge(parts, e + 1)
                dst = t["k_scr"] if which == "k" else t["q_scr"]
                sp.dma_start(dst[:, mt * P:(mt + 1) * P, hf * HALF:(hf + 1) * HALF].rearrange("c p t -> p c t"),
                             qk_parts[:, e % 2, :, :]).then_inc(parts_stored[e % 2], 16)
                if e == 3:
                    for b in range(2):
                        sp.wait_ge(parts_stored[b], 32)
                    sp.wait_ge(x_lo_s, KC)
                    sp.wait_ge(w_lo_s, KC)
                    load_stack(0, 0)
                if e == 7:
                    load_stack(1, 1)
                    sp.dma_start(xres[:], t["x"].rearrange("(n p) d -> p n d", p=P)).then_inc(xres_in, 16)
                    sp.dma_start(bo_all[:], t["bo"].rearrange("(a n) -> a n", a=1).to_broadcast([P, D])).then_inc(bo_in, 16)
            sp.wait_ge(proj, NKQ)
            sp.dma_start(wo_raw[:], t["wo"].rearrange("(c p) n -> p c n", p=P)).then_inc(wo_in, 16)
            for b in range(2):
                sp.wait_ge(parts_stored[b], 16 * NKQ // 2)
            mrows(0, 0)

            def group(g, c):
                sp.wait_ge(st_ready, NST * g + 1)
                load_stack((c + 2) % 3, g + 2)
                store_ctx(g, 0)
                mrows((c + 1) % 3, g + 1)
                store_ctx(g, 1)

            with sp.Fori(0, 2) as it:
                for c in range(3):
                    group(it * 3 + c, c)
            load_ctx(0)
            store_ctx(6, 0)
            load_ctx(1)
            mrows(1, 7)
            store_ctx(6, 1)
            load_ctx(2)
            store_ctx(7, 0)
            store_ctx(7, 1)
            load_ctx(3)
            with sp.Fori(0, TT) as tt:
                sp.wait_ge(ln_x, TT + tt + 1)
                sp.dma_start(t["out"][bass.ds(tt * P, P), :],
                             xres[:, bass.ds(tt, 1), :].rearrange("p a d -> p (a d)")).then_inc(out_s, 16)
            sp.wait_ge(out_s, 16 * TT)

        @block.gpsimd
        def _(pool):
            for m in (ident_f, ident_b, mask_q, mask_k):
                pool.memset(m[:], 0.0).then_inc(consts, 1)
            pool.memset(eps[:], EPS).then_inc(consts, 1)
            for b in range(3):
                pool.memset(v_ones[b][:, :, HD:32], 1.0).then_inc(consts, 1)
            pool.wait_ge(consts, 4)
            for m, op, fill, sign in ((ident_f, ALU.not_equal, 1.0, 1), (ident_b, ALU.not_equal, 1.0, 1),
                                      (mask_q, ALU.is_ge, NEG, 1), (mask_k, ALU.is_ge, NEG, -1)):
                pool.affine_select(out=m[:], in_=m[:], compare_op=op, fill=fill, base=0,
                                   pattern=[[-sign, P]], channel_multiplier=sign).then_inc(consts, 1)
            N_CONSTS = 12

            def right_add(n, i, buf=0):
                pool.wait_ge(line_ready, n * NLINE + i + 2)
                if i:
                    pool.wait_ge(right_sum, n * 3 + i)
                pool.tensor_tensor(lines[buf][:, R0, :], lines[buf][:, R0, :], lines[buf][:, R1 + i, :],
                                   ALU.add).then_inc(right_sum, 1)

            def weight(n, out, buf, k):
                pool.wait_ge(dq_code, n + 1)
                pool.wait_ge(scales_in[buf], 16 * (k + 1))
                pool.tensor_tensor(out, lines[buf][:, L0, :], scales[buf][:], ALU.mult).then_inc(dq_w, 1)

            def unit(n, out):
                L = lines[0]
                for i in range(3):
                    right_add(n, i)
                pool.wait_ge(dq_l0, n + 1)
                for i, src in enumerate((L1, L2, L3)):
                    pool.wait_ge(line_ready, n * NLINE + i + 5)
                    if i:
                        pool.wait_ge(left_pool, n * 3 + i)
                    pool.tensor_tensor(L[:, L0, :], L[:, L0, :], L[:, src, :], ALU.add).then_inc(left_pool, 1)
                pool.wait_ge(right_sum, n * 3 + 3)
                pool.wait_ge(left_pool, n * 3 + 3)
                pool.tensor_tensor(L[:, L0, :], L[:, R0, :], L[:, L0, :], ALU.subtract).then_inc(dq_code, 1)
                weight(n, out, 0, n)

            def stage_v(buf, g):
                pool.tensor_copy(v_ones[buf][:, :, 0:HD], v_all[:, :, bass.ds(g * HD, HD)]).then_inc(v_staged, 1)

            for n in range(EARLY_UNITS - 1):
                unit(n, unit_slot(n))
            pool.wait_ge(v_ready, 2)
            pool.wait_ge(consts, N_CONSTS)
            stage_v(0, 0)
            unit(EARLY_UNITS - 1, unit_slot(EARLY_UNITS - 1))
            pool.wait_ge(xres_in, 16)
            pool.wait_ge(bo_in, 16)
            pool.tensor_tensor(xres[:], xres[:], bo_all[:].unsqueeze(1).to_broadcast([P, TT, D]), ALU.add).then_inc(bo_added, 1)

            def group(g, c, n, count):
                pool.wait_ge(pv_done, NPV * g + 1)
                stage_v((c + 1) % 3, g + 1)
                for k in range(count):
                    unit(n + k, unit_slot(n + k))

            with pool.Fori(0, 2) as it:
                for c in range(3):
                    group(it * 3 + c, c, it * sum(LOOP_UNITS) + EARLY_UNITS + sum(LOOP_UNITS[:c]), LOOP_UNITS[c])
            pool.wait_ge(wo_lo_s, 1)
            group(6, 0, ATTN_UNITS - 4, 2)
            for n in (ATTN_UNITS - 2, ATTN_UNITS - 1):
                unit(n, unit_slot(n))
            pool.wait_ge(attn_out, TT)
            with pool.Fori(0, NW) as j:
                n = 2 * j + ATTN_UNITS
                for i in range(3):
                    right_add(n, i, 0)
                right_add(n + 1, 0, 1)
                weight(n, window_slot(j, 0), 0, j + ATTN_UNITS)
                for i in range(1, 3):
                    right_add(n + 1, i, 1)
                weight(n + 1, window_slot(j, 1), 1, j)

        @block.scalar
        def _(act):
            def load_codes(n, buf=0):
                act.dma_start(codes[buf][:], t["codes"][bass.ds(n, 1), :, :].rearrange("a p n -> (a p) n")).then_inc(codes_in[buf], 16)

            def load_scales(n, buf=0):
                act.dma_start(scales[buf][:], t["scales"][bass.ds(n, 1), :, :].rearrange("a b n -> (a b) n").unsqueeze(1)
                              .to_broadcast([2, BLOCK, UNIT])).then_inc(scales_in[buf], 16)

            def line_pass(n, k, buf=0, prev=1, ahead=1):
                if k == 0:
                    act.wait_ge(u_ready, n + 1)
                    if prev:
                        act.wait_ge(dq_w, n + 1 - prev)
                    load_scales(n, buf)
                    if ahead:
                        load_codes(n + ahead, buf)
                a, b = LINES[k]
                act.activation(lines[buf][:, k, :], us[buf][:], ACT.Relu, bias=b, scale=a).then_inc(line_ready, 1)

            def unit(n, buf=0, prev=1, ahead=1):
                for k in range(NLINE):
                    line_pass(n, k, buf, prev, ahead)

            act.sem_inc(ctx_evac, FREE)
            for hf in range(NH):
                act.sem_inc(ctx_stored[hf], 16 * FREE)
            load_codes(0)
            for kc in range(KC):
                act.wait_ge(xT_in[kc], 16)
                act.activation(xT_hi[:, kc, :], xT_raw[:, kc, :], ACT.Copy).then_inc(x_hi_s, 1)
                act.wait_ge(w_in[kc], 16)
                act.activation(w_hi[:, kc, :], w_raw[:, kc, :], ACT.Copy).then_inc(w_hi_s, 1)
            for e in range(NKQ):
                act.wait_ge(proj, e + 1)
                if e >= 2:
                    act.wait_ge(parts_stored[e % 2], 16 * (e // 2))
                act.activation(qk_parts[:, e % 2, 0, :], ps[:, e % 4, :], ACT.Copy).then_inc(part_h, 1)
                if e == 3:
                    unit(0, prev=0)
                    for hf in range(NH):
                        act.wait_ge(v_proj, hf + 1)
                        act.activation(v_all[:, 4 * hf:4 * hf + 4, :], ps[:, 6 + hf, :], ACT.Copy).then_inc(v_ready, 1)
                if e == 7:
                    unit(1)
            unit(2)
            act.wait_ge(wo_in, 16)
            act.activation(wo_hi[:], wo_raw[:], ACT.Copy).then_inc(wo_hi_s, 1)
            unit(3)

            def evac(g, hf):
                act.wait_ge(pv_done, NPV * g + (4 if hf == 0 else NPV))
                act.wait_ge(ctx_stored[hf], 16 * (g + FREE))
                act.activation(ctx_raw[:, hf, :], ps[:, B_CTX, :], ACT.Copy).then_inc(ctx_evac, 1)

            def split_ctx(ch):
                act.wait_ge(ctx_mul, ch + 1)
                act.activation(ctx_hi[:, ch, :], rsum_in[:], ACT.Copy).then_inc(ctx_hi_s, 1)

            def group(g, n, count, chunks=()):
                at_step = [5 + i for i in range(NLINE)] + [17 + i for i in range(NLINE)]
                for s, (qh, kt, pr) in enumerate(STEPS):
                    w = (qh + 1) * HALF - q_from(qh, kt)
                    act.wait_ge(st_ready, NST * g + s + 1)
                    if s >= 4:
                        act.wait_ge(pv_done, NPV * g + (s - 4) // 2 + 1)
                    act.activation(probs[:, s % 4, :, 0:w], ps[:, 2 * (s % 2):2 * (s % 2) + 2, 0:w], ACT.Exp,
                                   scale=SCALE).then_inc(exp_done, 1)
                    if s == 9:
                        evac(g, 0)
                    if s in at_step and at_step.index(s) < NLINE * count:
                        k = at_step.index(s)
                        line_pass(n + k // NLINE, k % NLINE)
                    for ch, step in chunks:
                        if s == step:
                            split_ctx(ch)
                evac(g, 1)

            with act.Fori(0, 2) as it:
                for c in range(3):
                    group(it * 3 + c, it * sum(LOOP_UNITS) + EARLY_UNITS + sum(LOOP_UNITS[:c]), LOOP_UNITS[c])
            group(6, ATTN_UNITS - 4, 2, chunks=((0, 10), (1, 20)))
            group(7, ATTN_UNITS - 2, 2, chunks=((2, 12),))
            split_ctx(3)

            def std(n, slot):
                act.wait_ge(ln_ag, n + 1)
                act.activation(ln_std[:, slot, :], ln_mv[:, slot, 1:2], ACT.Sqrt, bias=eps[:]).then_inc(ln_sd, 1)

            def normalise(n, tt, slot):
                act.wait_ge(ln_b, n + 1)
                x_tt = xres[:, bass.ds(tt, 1), :].rearrange("p a d -> p (a d)")
                act.activation(x_tt, x_tt, ACT.Identity, bias=ln_nb[:, slot, :], scale=ln_rstd[:, slot, :]).then_inc(ln_x, 1)

            for tt in range(TT + 2):
                if tt < TT:
                    std(tt, tt % 4)
                if 1 <= tt <= TT:
                    normalise(tt - 1, tt - 1, (tt - 1) % 4)
                if tt >= 2:
                    act.wait_ge(x1T_ps, tt - 1)
                    act.activation(x1T_hi[:, :, (tt - 2) * P:(tt - 1) * P],
                                   ps[:, tt - 2, :].rearrange("p (c n) -> p c n", c=KC), ACT.Copy).then_inc(x1T_hi_s, 1)
            load_codes(ATTN_UNITS + 1, 1)

            def silu(j, par):
                act.wait_ge(gate_up, 2 * j + 1)
                act.activation(hid[:, bass.ds(j, 1), :].rearrange("p a n -> p (a n)"),
                               ps[:, 4 * par:4 * par + 2, :].rearrange("p a n -> p (a n)"), ACT.Silu).then_inc(silu_s, 1)

            def window(j, par, first=False, ahead=2):
                if not first:
                    act.wait_ge(gu_lo_s, j)
                    silu(j - 1, 1 - par)
                n = 2 * j + ATTN_UNITS
                unit(n, 0, 1 if first else 2, ahead)
                unit(n + 1, 1, 0 if first else 2, ahead)

            window(0, 0, first=True)
            with act.Fori(1, NW - 2, 2) as j:
                window(j, 1)
                window(j + 1, 0)
            window(NW - 1, 1, ahead=0)
            for j in range(NW - 1, MT):
                act.wait_ge(gu_lo_s, j + 1)
                silu(j, j % 2)
                if j == NW - 1:
                    act.wait_ge(dq_w, UNITS)
                half = MT // 2 * (j - NW + 1)
                for i in range(half, min(half + MT // 2, MT)):
                    act.activation(wd_hi[:, i, :], w_down[:, i, :], ACT.Copy).then_inc(wd_hi_s, 1)

            def split_hidden(tt, par):
                act.activation(hid_hi[par][:], hid[:, :, bass.ds(tt * P, P)], ACT.Copy).then_inc(hh_s, 1)

            def out_tile(tt, par, more=True):
                if more:
                    act.wait_ge(down, tt + 1)
                    split_hidden(tt + 2, par)
                std(tt + TT, par)
                normalise(tt + TT, tt, par)

            act.wait_ge(hid_s, MT)
            split_hidden(0, 0)
            split_hidden(1, 1)
            with act.Fori(0, TT - 3, 2) as tt:
                for par in range(2):
                    out_tile(tt + par, par)
            for par in range(2):
                out_tile(TT - 2 + par, par, more=False)

        @block.vector
        def _(dve):
            def u_of(n, buf, k, prev):
                dve.wait_ge(codes_in[buf], 16 * (k + 1))
                if prev:
                    dve.wait_ge(line_ready, (n + 1 - prev) * NLINE)
                    dve.wait_ge(dq_l0, n + 1 - prev)
                dve.tensor_scalar(us[buf][:], codes[buf][:], float(-ZERO_AT), None, ALU.add).then_inc(u_ready, 1)

            def first_left(n, buf, prev):
                dve.wait_ge(u_ready, n + 1)
                if prev:
                    dve.wait_ge(dq_w, n + 1 - prev)
                dve.tensor_scalar(lines[buf][:, L0, :], us[buf][:], SLOPE_L0, 0.0, ALU.mult, ALU.max).then_inc(dq_l0, 1)

            def make_u(n, prev=1):
                u_of(n, 0, n, prev)
                first_left(n, 0, prev)

            for b in range(3):
                dve.memset(k_stack[b][MROW:STACKM, :], 1.0).then_inc(k_ones, 1)
            for kc in range(KC):
                dve.wait_ge(x_hi_s, kc + 1)
                dve.tensor_tensor(xT_lo[:, kc, :], xT_raw[:, kc, :], xT_hi[:, kc, :].bitcast(F32), ALU.subtract).then_inc(x_lo_s, 1)
                dve.wait_ge(w_hi_s, kc + 1)
                dve.tensor_tensor(w_lo[:, kc, :], w_raw[:, kc, :], w_hi[:, kc, :].bitcast(F32), ALU.subtract).then_inc(w_lo_s, 1)
            make_u(0, prev=0)

            def evac_parts(e):
                dve.wait_ge(part_h, e + 1)
                if e >= 1:
                    dve.wait_ge(parts, e)
                dve.tensor_tensor(resid[:], ps[:, e % 4, :], qk_parts[:, e % 2, 0, :], ALU.subtract).then_inc(part_r, 1)
                dve.wait_ge(part_r, e + 1)
                dve.tensor_copy(qk_parts[:, e % 2, 1, :], resid[:]).then_inc(part_m, 1)
                dve.wait_ge(part_m, e + 1)
                dve.tensor_tensor(qk_parts[:, e % 2, 2, :], resid[:], qk_parts[:, e % 2, 1, :], ALU.subtract).then_inc(parts, 1)

            def reduce(idx, k, buf):
                i, kh, r = MAX_TILES[k]
                n = width(i, kh)
                dve.wait_ge(max_scores, idx + 1)
                dst = row_max[:, buf, r * TT + i:r * TT + i + 1] if kh == 0 else row_max_hi[:, r, i - 4:i - 3]
                dve.reduce_max(dst, ps[:, B_MAX + k % 2, 0:n], AX.X).then_inc(max_done, 1)

            def combine(g, buf):
                dve.wait_ge(max_done, NMAX * g + NMAX)
                v = row_max[:, buf, :].rearrange("p (r i) -> p r i", r=REP)[:, :, 4:8]
                dve.tensor_tensor(v, v, row_max_hi[:], ALU.max).then_inc(max_all, 1)

            def negate(g, first=False):
                dve.wait_ge(max_T, g + 1)
                if not first:
                    dve.wait_ge(mrow_in, 48 * g)
                tr = ps[0:32, B_TR, 0:P]
                dve.tensor_scalar(neg_max[:, 0, :], tr, -1.0, None, ALU.mult).then_inc(nm_h, 1)
                dve.wait_ge(nm_h, g + 1)
                dve.scalar_tensor_tensor(neg_max_f[:], tr, -1.0, neg_max[:, 0, :], ALU.mult, ALU.subtract).then_inc(nm_r, 1)
                dve.wait_ge(nm_r, g + 1)
                dve.tensor_copy(neg_max[:, 1, :], neg_max_f[:]).then_inc(nm_m, 1)
                dve.wait_ge(nm_m, g + 1)
                dve.tensor_tensor(neg_max[:, 2, :], neg_max_f[:], neg_max[:, 1, :], ALU.subtract).then_inc(nm_all, 1)

            early = 0
            for e in range(NKQ):
                if e >= NKQ - 4:
                    for _ in range(EARLY_MAX):
                        reduce(early, early, 0)
                        early += 1
                evac_parts(e)
                if e == NKQ - 4:
                    make_u(1)
            for k in range(early, NMAX):
                reduce(k, k, 0)
                if k == early + 4:
                    make_u(2)
            combine(0, 0)
            negate(0, first=True)
            dve.wait_ge(wo_hi_s, 1)
            dve.tensor_tensor(wo_lo[:], wo_raw[:], wo_hi[:].bitcast(F32), ALU.subtract).then_inc(wo_lo_s, 1)
            for k in range(LEAD):
                reduce(NMAX + k, k, 1)
            make_u(3)

            def invert_sums(ch):
                dve.wait_ge(sums_in, 16 * (ch + 1))
                dve.reciprocal(sums[:], sums[:]).then_inc(sums_inv, 1)

            def scale_ctx(ch):
                dve.wait_ge(ctx_loaded, 16 * (ch + 1))
                dve.wait_ge(rsum_loaded, 16 * (ch + 1))
                dve.tensor_tensor(rsum_in[:], ctx_in[:], rsum_in[:], ALU.mult).then_inc(ctx_mul, 1)

            def ctx_low(ch):
                dve.wait_ge(ctx_hi_s, ch + 1)
                dve.tensor_tensor(ctx_lo[:, ch, :], rsum_in[:], ctx_hi[:, ch, :].bitcast(F32), ALU.subtract).then_inc(ctx_lo_s, 1)

            def group(g, c, n, units, count=NMAX, before={}):
                for s in range(count):
                    k = (LEAD + s) % NMAX
                    if s in before:
                        before[s]()
                    if s == 9:
                        make_u(n)
                    if s == 31 and units == 2:
                        make_u(n + 1)
                    if s == 0:
                        dve.wait_ge(max_all, g + 1)
                    reduce(NMAX * (g + 1) + LEAD + s, k, (c + 1 + (LEAD + s) // NMAX) % 3)
                    if s == NMAX - LEAD - 1:
                        combine(g + 1, (c + 1) % 3)
                    if s == NMAX - LEAD + 1:
                        negate(g + 1)
                if count == NMAX - LEAD:
                    negate(g + 1)

            with dve.Fori(0, 2) as it:
                for c in range(3):
                    group(it * 3 + c, c, it * sum(LOOP_UNITS) + EARLY_UNITS + sum(LOOP_UNITS[:c]), LOOP_UNITS[c])
            group(6, 0, ATTN_UNITS - 4, 2, count=NMAX - LEAD, before={
                4: lambda: invert_sums(0), 16: lambda: scale_ctx(0), 22: lambda: ctx_low(0),
                26: lambda: invert_sums(1), 34: lambda: scale_ctx(1)})
            ctx_low(1)
            make_u(ATTN_UNITS - 2)
            invert_sums(2)
            scale_ctx(2)
            ctx_low(2)
            make_u(ATTN_UNITS - 1)

            def split_gate_up(j, par):
                slot = hid[:, bass.ds(j, 1), :].rearrange("p a n -> p (a n)")
                dve.wait_ge(dq_w, 2 * j + MT + 2)
                dve.tensor_copy(gu_hi[:, par, :], slot).then_inc(gu_hi_s, 1)
                dve.wait_ge(gu_hi_s, j + 1)
                dve.tensor_tensor(gu_lo[:, par, :], slot, gu_hi[:, par, :].bitcast(F32), ALU.subtract).then_inc(gu_lo_s, 1)

            dve.wait_ge(pv_done, NPV * G)
            split_gate_up(0, 0)
            invert_sums(3)
            split_gate_up(1, 1)
            scale_ctx(3)
            ctx_low(3)

            def ln_front(n, tt, src, slot):
                x_tt = xres[:, bass.ds(tt, 1), :].rearrange("p a d -> p (a d)")
                dve.tensor_tensor(x_tt, src, x_tt, ALU.add).then_inc(ln_y, 1)
                dve.wait_ge(ln_y, n + 1)
                dve.bn_stats(ln_stats[:, slot % 2, :], x_tt).then_inc(ln_st, 1)
                dve.wait_ge(ln_st, n + 1)
                dve.bn_aggr(ln_mv[:, slot, :], ln_stats[:, slot % 2, :]).then_inc(ln_ag, 1)

            def ln_back(n, slot):
                dve.wait_ge(ln_sd, n + 1)
                dve.reciprocal(ln_rstd[:, slot, :], ln_std[:, slot, :]).then_inc(ln_rs, 1)
                dve.wait_ge(ln_rs, n + 1)
                dve.scalar_tensor_tensor(ln_nb[:, slot, :], ln_mv[:, slot, 0:1], -1.0, ln_rstd[:, slot, :],
                                         ALU.mult, ALU.mult).then_inc(ln_b, 1)

            dve.wait_ge(bo_added, 1)
            for tt in range(TT + 2):
                if tt < TT:
                    dve.wait_ge(attn_out, tt + 1)
                    if tt >= 4:
                        dve.wait_ge(ln_x, tt - 3)
                    ln_front(tt, tt, ps[:, tt, :], tt % 4)
                if 1 <= tt <= TT:
                    ln_back(tt - 1, (tt - 1) % 4)
                if tt >= 2:
                    dve.wait_ge(x1T_hi_s, tt - 1)
                    dve.tensor_tensor(x1T_lo[:, :, (tt - 2) * P:(tt - 1) * P],
                                      ps[:, tt - 2, :].rearrange("p (c n) -> p c n", c=KC),
                                      x1T_hi[:, :, (tt - 2) * P:(tt - 1) * P].bitcast(F32), ALU.subtract).then_inc(x1T_lo_s, 1)

            def hidden_product(j, par):
                dve.wait_ge(gate_up, 2 * j + 2)
                dve.wait_ge(silu_s, j + 1)
                slot = hid[:, bass.ds(j, 1), :].rearrange("p a n -> p (a n)")
                dve.tensor_tensor(slot, slot, ps[:, 4 * par + 2:4 * par + 4, :].rearrange("p a n -> p (a n)"),
                                  ALU.mult).then_inc(hid_s, 1)

            def left_sum(n, buf, i, done):
                dve.wait_ge(line_ready, n * NLINE + i + 5)
                if i:
                    dve.wait_ge(left_dve, done + i)
                else:
                    dve.wait_ge(dq_l0, n + 1)
                dve.tensor_tensor(lines[buf][:, L0, :], lines[buf][:, L0, :], lines[buf][:, L1 + i, :],
                                  ALU.add).then_inc(left_dve, 1)

            def code_of(n, buf, done):
                dve.wait_ge(left_dve, done + 3)
                dve.wait_ge(right_sum, n * 3 + 3)
                dve.tensor_tensor(lines[buf][:, L0, :], lines[buf][:, R0, :], lines[buf][:, L0, :],
                                  ALU.subtract).then_inc(dq_code, 1)

            def window(j, par, first=False):
                n, prev = 2 * j + ATTN_UNITS, 1 if first else 2
                if not first:
                    hidden_product(j - 1, 1 - par)
                    split_gate_up(j + 1, 1 - par)
                u_of(n, 0, j + ATTN_UNITS, prev)
                u_of(n + 1, 1, j, 0 if first else prev)
                first_left(n, 0, prev)
                first_left(n + 1, 1, 0 if first else prev)
                for which in range(2):
                    for i in range(3):
                        left_sum(n + which, which, i, 6 * j + 3 * which)
                    code_of(n + which, which, 6 * j + 3 * which)

            window(0, 0, first=True)
            with dve.Fori(1, NW - 2, 2) as j:
                window(j, 1)
                window(j + 1, 0)
            window(NW - 1, 1)
            hidden_product(NW - 1, 1)
            split_gate_up(NW + 1, 1)
            hidden_product(NW, 0)
            hidden_product(NW + 1, 1)

            def down_low(j):
                dve.wait_ge(wd_hi_s, j + 1)
                dve.tensor_tensor(wd_lo[:, j, :], w_down[:, j, :], wd_hi[:, j, :].bitcast(F32), ALU.subtract).then_inc(wd_lo_s, 1)

            def hidden_low(tt, par):
                dve.wait_ge(hh_s, tt + 1)
                dve.tensor_tensor(hid_lo[par][:], hid[:, :, bass.ds(tt * P, P)], hid_hi[par][:].bitcast(F32),
                                  ALU.subtract).then_inc(hl_s, 1)

            for j in range(2):
                down_low(j)
            hidden_low(0, 0)
            for j in range(2, MT):
                down_low(j)
            hidden_low(1, 1)

            def out_tile(tt, par, more=True):
                dve.wait_ge(down, tt + 1)
                dve.wait_ge(ln_x, tt + TT - 1)
                ln_front(tt + TT, tt, ps[:, par, :], par)
                if more:
                    hidden_low(tt + 2, par)
                ln_back(tt + TT, par)

            for tt in range(TT):
                out_tile(tt, tt % 2, more=tt < TT - 2)

        @block.tensor
        def _(pe):
            def three_pass(out, a_hi, a_lo, b_hi, b_lo, chunks, start=True, stop=True):
                mm, n, at_ = None, 3 * len(chunks), 0
                for c in chunks:
                    for a, b in ((a_hi, b_hi), (a_hi, b_lo), (a_lo, b_hi)):
                        mm = pe.matmul(out, a(c), b(c), start=start and at_ == 0, stop=stop and at_ == n - 1)
                        at_ += 1
                return mm

            def max_tile(idx, k, buf, free=True):
                i, kh, r = MAX_TILES[k]
                n = width(i, kh)
                bank = B_MAX + k % 2
                diag = n < HALF or (i + 1) * P == (kh + 1) * HALF
                if free:
                    pe.wait_ge(max_done, idx - 1)
                mm = pe.matmul(ps[:, bank, 0:n], q_stack[buf][0:STACK, r * T + i * P:r * T + (i + 1) * P],
                               k_stack[buf][0:STACK, kh * HALF:kh * HALF + n], start=True, stop=not diag)
                if diag:
                    mm = pe.matmul(ps[:, bank, n - P:n], ident_b[:], mask_q[:], start=False, stop=True)
                mm.then_inc(max_scores, 1)

            def project(e, chunks):
                which, mt, hf = KQ[e]
                col = 4 * P if which == "k" else mt * P
                return three_pass(ps[:, e % 4, :], lambda c: w_hi[:, c, col:col + P], lambda c: w_lo[:, c, col:col + P],
                                  lambda c: xT_hi[:, c, hf * HALF:(hf + 1) * HALF],
                                  lambda c: xT_lo[:, c, hf * HALF:(hf + 1) * HALF], chunks,
                                  start=chunks[0] == 0, stop=chunks[-1] == KC - 1)

            for kc in range(KC):
                pe.wait_ge(x_lo_s, kc + 1)
                pe.wait_ge(w_lo_s, kc + 1)
                for e in range(4):
                    mm = project(e, [kc])
                    if kc == KC - 1:
                        mm.then_inc(proj, 1)
            for hf in range(NH):
                for q4 in range(4):
                    tok = (4 * hf + q4) * P
                    mm = three_pass(ps[:, 6 + hf, q4 * P:(q4 + 1) * P], lambda c: xT_hi[:, c, tok:tok + P],
                                    lambda c: xT_lo[:, c, tok:tok + P], lambda c: w_hi[:, c, 5 * P:6 * P],
                                    lambda c: w_lo[:, c, 5 * P:6 * P], range(KC))
                mm.then_inc(v_proj, 1)
            early = 0
            for e in range(4, NKQ):
                pe.wait_ge(part_r, e - 3)
                if e < NKQ - 4:
                    project(e, range(KC)).then_inc(proj, 1)
                    continue
                if e == NKQ - 4:
                    pe.wait_ge(consts, 12)
                    pe.wait_ge(k_ones, 3)
                for half in range(2):
                    mm = project(e, range(2 * half, 2 * half + 2))
                    if half == 1:
                        mm.then_inc(proj, 1)
                    if e == NKQ - 4 and half == 0:
                        pe.wait_ge(stack_in[0], 192)
                    for _ in range(EARLY_MAX // 2):
                        max_tile(early, early, 0, free=early >= 2)
                        early += 1

            def transpose_max(g, buf, first=False):
                pe.wait_ge(max_all, g + 1)
                if not first:
                    pe.wait_ge(nm_all, g)
                pe.transpose(ps[0:32, B_TR, 0:P], row_max[:, buf, :], ident_f[:]).then_inc(max_T, 1)

            def score_step(g, s, buf):
                qh, kt, pr = STEPS[s]
                q0 = q_from(qh, kt)
                n = (qh + 1) * HALF - q0
                diag = q0 == kt * P
                if s >= 2:
                    pe.wait_ge(exp_done, NST * g + s - 1)
                for a in range(2):
                    r = 2 * pr + a
                    bank = 2 * (s % 2) + a
                    mm = pe.matmul(ps[:, bank, 0:n], k_stack[buf][0:STACKM, kt * P:(kt + 1) * P],
                                   q_stack[buf][0:STACKM, r * T + q0:r * T + q0 + n], start=True, stop=not diag)
                    if diag:
                        mm = pe.matmul(ps[:, bank, 0:P], ident_b[:], mask_k[:], start=False, stop=True)
                mm.then_inc(st_ready, 1)

            def pv(g, m, buf):
                qh, kt, _ = STEPS[2 * m]
                off = q_from(qh, kt) - qh * HALF
                n = HALF - off
                pe.wait_ge(exp_done, NST * g + 2 * m + 2)
                if m == 0:
                    pe.wait_ge(ctx_evac, NH * g + FREE)
                if m == 4:
                    pe.wait_ge(ctx_evac, NH * g + 1 + FREE)
                for r in range(REP):
                    s = 2 * m + r // 2
                    mm = pe.matmul(ps[32 * r:32 * r + 32, B_CTX, off:HALF], v_ones[buf][:, kt, :],
                                   probs[:, s % 4, r % 2, 0:n], start=kt == 0, stop=kt == 4 * (qh + 1) - 1)
                mm.then_inc(pv_done, 1)

            pe.wait_ge(v_ready, 2)
            for k in range(early, NMAX):
                max_tile(k, k, 0)
            pe.wait_ge(part_r, NKQ)
            pe.wait_ge(stack_in[1], 192)
            for k in range(LEAD):
                max_tile(NMAX + k, k, 1)
                if k == 1:
                    transpose_max(0, 0, first=True)

            def group(g, it, c, count=NMAX):
                pe.wait_ge(mrow_in, 48 * (g + 1))
                pe.wait_ge(v_staged, g + 1)
                for s in range(NST):
                    score_step(g, s, c)
                    for k in (2 * s, 2 * s + 1):
                        if k >= count:
                            continue
                        if k == NMAX - LEAD:
                            pe.wait_ge(stack_in[(c + 2) % 3], 192 * (it + (c + 2) // 3 + 1))
                        max_tile(NMAX * (g + 1) + LEAD + k, (LEAD + k) % NMAX, (c + 1 + (LEAD + k) // NMAX) % 3)
                        if k == NMAX - LEAD + 1 or (k == count - 1 and count == NMAX - LEAD):
                            transpose_max(g + 1, (c + 1) % 3)
                    if s >= 2 and s % 2 == 0:
                        pv(g, s // 2 - 1, c)
                pv(g, NPV - 1, c)

            with pe.Fori(0, 2) as it:
                for c in range(3):
                    group(it * 3 + c, it, c)
            group(6, 2, 0, count=NMAX - LEAD)
            group(7, 2, 1, count=0)

            def wo_tile(tt, chunks):
                return three_pass(ps[:, tt, :], lambda c: ctx_hi[:, c, tt * P:(tt + 1) * P],
                                  lambda c: ctx_lo[:, c, tt * P:(tt + 1) * P], lambda c: wo_hi[:, c, :],
                                  lambda c: wo_lo[:, c, :], chunks, start=chunks[0] == 0, stop=chunks[-1] == KC - 1)

            def x1_transpose(tt):
                pe.wait_ge(ln_x, tt + 1)
                for c in range(KC):
                    mm = pe.transpose(ps[:, tt, c * P:(c + 1) * P], xres[:, tt, c * P:(c + 1) * P], ident_f[:])
                mm.then_inc(x1T_ps, 1)

            pe.wait_ge(wo_lo_s, 1)
            pe.wait_ge(ctx_lo_s, KC - 1)
            pe.wait_ge(exp_done, NST * G)
            pe.wait_ge(max_done, NMAX * G)
            pe.wait_ge(nm_all, G)
            for tt in range(TT):
                if tt == B_CTX:
                    pe.wait_ge(ctx_evac, NH * G + FREE)
                wo_tile(tt, range(KC - 1))
            pe.wait_ge(ctx_lo_s, KC)
            for tt in range(TT):
                wo_tile(tt, range(KC - 1, KC)).then_inc(attn_out, 1)

            def gate_or_up(par, which, hf):
                return three_pass(ps[:, 4 * par + 2 * which + hf, :],
                                  lambda c: gu_hi[:, par, which * UNIT + c * P:which * UNIT + (c + 1) * P],
                                  lambda c: gu_lo[:, par, which * UNIT + c * P:which * UNIT + (c + 1) * P],
                                  lambda c: x1T_hi[:, c, hf * HALF:(hf + 1) * HALF],
                                  lambda c: x1T_lo[:, c, hf * HALF:(hf + 1) * HALF], range(KC))

            for tt in range(4):
                x1_transpose(tt)
            for j in range(2):
                pe.wait_ge(gu_lo_s, j + 1)
                for which in range(2):
                    x1_transpose(4 + 2 * j + which)
                    pe.wait_ge(x1T_lo_s, (4, 4, 5, 7)[2 * j + which])
                    gate_or_up(j, which, 0)
            pe.wait_ge(x1T_lo_s, TT)
            for j in range(2):
                for which in range(2):
                    gate_or_up(j, which, 1).then_inc(gate_up, 1)
            with pe.Fori(2, MT - 1, 2) as j:
                for par in range(2):
                    pe.wait_ge(hid_s, j + par - 1)
                    pe.wait_ge(gu_lo_s, j + par + 1)
                    for which in range(2):
                        for hf in range(NH):
                            mm = gate_or_up(par, which, hf)
                        mm.then_inc(gate_up, 1)

            pe.wait_ge(hid_s, MT)
            with pe.Fori(0, TT - 1, 2) as tt:
                for par in range(2):
                    pe.wait_ge(hl_s, tt + par + 1)
                    pe.wait_ge(ln_y, tt + par + TT - 1)
                    for j in range(MT):
                        pe.wait_ge(wd_lo_s, j + 1)
                        for p3, (a, b) in enumerate(((hid_hi, wd_hi), (hid_hi, wd_lo), (hid_lo, wd_hi))):
                            mm = pe.matmul(ps[:, par, :], a[par][:, j, :], b[:, j, :],
                                           start=j == 0 and p3 == 0, stop=j == MT - 1 and p3 == 2)
                    mm.then_inc(down, 1)


def kernel(L0_attn_x, L0_attn_Wq, L0_attn_Wkv, L0_attn_Wo, L0_attn_bo, L0_ffn_gate_q, L0_ffn_gate_absmax,
           L0_ffn_up_q, L0_ffn_up_absmax, L0_ffn_down_q, L0_ffn_down_absmax):
    import concourse.bacc as bacc
    from concourse.bass_utils import run_bass_kernel_spmd

    x = np.asarray(L0_attn_x)[0]
    wq = np.asarray(L0_attn_Wq).reshape(D, G, REP, HD).transpose(0, 1, 3, 2).reshape(D, D)
    wkv = np.asarray(L0_attn_Wkv).reshape(D, G, 2, HD).transpose(0, 2, 1, 3).reshape(D, 2 * G * HD)

    def wide(q):
        return np.asarray(q).reshape(MT, P, KC, P).transpose(0, 3, 2, 1).reshape(MT, P, UNIT)

    def wide_scale(a):
        return np.asarray(a).reshape(MT, P, KC, 2).transpose(0, 3, 2, 1).reshape(MT, 2, UNIT)

    gate_up = np.stack([wide(L0_ffn_gate_q), wide(L0_ffn_up_q)], 1).reshape(2 * MT, P, UNIT)
    gate_up_s = np.stack([wide_scale(L0_ffn_gate_absmax), wide_scale(L0_ffn_up_absmax)], 1).reshape(2 * MT, 2, UNIT)
    down = np.asarray(L0_ffn_down_q).T.reshape(MT, P, UNIT)
    down_s = np.asarray(L0_ffn_down_absmax).reshape(D, 2 * MT).T.reshape(MT, 2, UNIT)
    arrays = {
        "x": x, "xT": x.T, "w_qkv": np.concatenate([wq, wkv], 1), "wo": np.asarray(L0_attn_Wo),
        "bo": np.asarray(L0_attn_bo),
        "codes": np.concatenate([down, gate_up], 0), "scales": np.concatenate([down_s, gate_up_s], 0),
    }
    arrays = {k: np.ascontiguousarray(v) for k, v in arrays.items()}
    nc = bacc.Bacc("TRN2", target_bir_lowering=False, num_devices=1)
    t = {k: nc.dram_tensor(k, list(v.shape), mybir.dt.from_np(v.dtype), kind="ExternalInput").ap()
         for k, v in arrays.items()}
    t["q_scr"] = nc.dram_tensor("q_scr", [3, D, T], BF16, kind="Internal").ap()
    t["k_scr"] = nc.dram_tensor("k_scr", [3, P, T], BF16, kind="Internal").ap()
    t["ctx_scr"] = nc.dram_tensor("ctx_scr", [G, P, T], F32, kind="Internal").ap()
    t["rsum_scr"] = nc.dram_tensor("rsum_scr", [KC, 2 * REP, T], F32, kind="Internal").ap()
    t["out"] = nc.dram_tensor("out", [T, D], F32, kind="ExternalOutput").ap()
    build_program(nc, t)
    r = run_bass_kernel_spmd(nc, [arrays], core_ids=[0])
    return np.asarray(r.results[0]["out"]).reshape(1, T, D)
```

```python
from contextlib import ExitStack

import numpy as np

import concourse.bass as bass
import concourse.mybir as mybir

F32, F32R, BF16, I32 = mybir.dt.float32, mybir.dt.float32r, mybir.dt.bfloat16, mybir.dt.int32
ALU, ACT, AX = mybir.AluOpType, mybir.ActivationFunctionType, mybir.AxisListType

P = 128
T, D, H, G = 1024, 512, 32, 8
HD = D // H
REP = H // G
KC = D // P
TT = T // P
HALF, NH = 512, T // 512
M = 1792
MT = M // P
BLOCK = 64
UNIT = 512
UNITS = 3 * MT
EPS = 1e-5
NEG = -3.0e38
SCALE = 1.0 / HD ** 0.5

Q_PART = (0, 0, 0, 1, 1, 2)
K_PART = (0, 1, 2, 0, 1, 0)
STACK = HD * len(Q_PART)
MROW = STACK
STACKM = STACK + 3

CODE = np.array([-1.0, -0.6961928009986877, -0.5250730514526367, -0.39491748809814453,
                 -0.28444138169288635, -0.18477343022823334, -0.09105003625154495, 0.0,
                 0.07958029955625534, 0.16093020141124725, 0.24611230194568634, 0.33791524171829224,
                 0.44070982933044434, 0.5626170039176941, 0.7229568362236023, 1.0], np.float32)
ZERO_AT = 7


def hinges(side, starts):
    def fma(a, u, b):
        return np.float32(np.float64(a) * u + np.float64(b))

    def ulps(v, n):
        return (np.array([v], np.float32).view(np.int32) + np.int32(n)).view(np.float32)[0]

    want = {v: side * CODE[ZERO_AT + side * v] for v in range(1 + (8 if side > 0 else 7))}
    total, terms = {v: np.float32(0) for v in want}, []

    def search(v0):
        pts = [v for v in (v0, v0 + 1) if v in want]
        rest = [np.float64(want[v]) - np.float64(total[v]) for v in pts]
        slope = np.float32(rest[1] - rest[0] if len(pts) == 2 else 2 * rest[0])
        for da in sorted(range(-400, 401), key=abs):
            a = ulps(slope, da)
            for db in range(-3, 4):
                b = ulps(np.float32(rest[0] - np.float64(a) * v0), db) if v0 else np.float32(0)
                if (all(total[v] + max(fma(a, v, b), np.float32(0)) == want[v] for v in pts)
                        and all(fma(a, v, b) <= 0 for v in range(-8, v0))):
                    return a, b
        raise ValueError(v0)

    for v0 in starts:
        a, b = search(v0)
        terms.append((float(side * a), float(b)))
        for v in want:
            total[v] = total[v] + max(fma(a, v, b), np.float32(0))
    return terms


RIGHT, LEFT = hinges(1, (1, 3, 5, 7)), hinges(-1, (0, 2, 4, 6))
R0, R1, R2, R3, L1, L2, L3, L0 = range(8)
NLINE = 7
LINES = RIGHT + LEFT[1:]
SLOPE_L0 = LEFT[0][0]

LEAD = 12
MAX_TILES = [(i, kh, r) for i, kh in [(1, 0), (0, 0), (3, 0), (2, 0), (5, 1), (4, 1), (4, 0), (5, 0), (6, 0),
                                      (7, 0), (7, 1), (6, 1)] for r in range(REP)]
NMAX = len(MAX_TILES)
STEPS = [(qh, kt, pr) for qh in range(NH) for kt in range(4 * (qh + 1)) for pr in range(2)]
NST = len(STEPS)
NPV = NST // 2
TR_STEP = (NMAX - LEAD) // 2

EARLY_UNITS = 4
LOOP_UNITS = (2, 2, 1)
LATE = EARLY_UNITS + 2 * sum(LOOP_UNITS)
ATTN_UNITS = LATE + 6
NW = (UNITS - ATTN_UNITS) // 2
FREE = 1


def width(i, kh):
    return min(HALF, (i + 1) * P - kh * HALF)


def q_from(qh, kt):
    return max(qh * HALF, kt * P)


def build_program(nc, t):
    ctx = ExitStack()
    with ctx:
        base = (nc.sbuf_base + 63) // 64 * 64

        def at(name, kib, shape, dt):
            return nc.alloc_sbuf_tensor_at(name, shape, dt, offset=base + int(kib * 1024))

        xres = at("xres", 0, [P, TT, D], F32)
        ident_f = at("ident_f", 16, [P, P], F32)
        ident_b = at("ident_b", 16.5, [P, P], BF16)
        mask_q = at("mask_q", 16.75, [P, P], BF16)
        mask_k = at("mask_k", 17, [P, P], BF16)
        row_max = at("row_max", 17.25, [P, 3, 32], F32)
        row_max_hi = at("row_max_hi", 17.625, [P, REP, 4], F32)
        eps = at("eps", 17.6875, [P, 1], F32)
        ln_stats = at("ln_stats", 17.71875, [P, 2, 6], F32)
        ln_mv = at("ln_mv", 17.78125, [P, 4, 2], F32)
        ln_std = at("ln_std", 17.8125, [P, 4, 1], F32)
        ln_rstd = at("ln_rstd", 17.84375, [P, 4, 1], F32)
        ln_nb = at("ln_nb", 17.875, [P, 4, 1], F32)
        w_down = at("w_down", 18, [P, MT, UNIT], F32)
        codes = [at("codes_a", 46, [P, UNIT], I32), at("codes_b", 67, [P, UNIT], I32)]
        scales = [at("scales_a", 48, [P, UNIT], F32), at("scales_b", 69, [P, UNIT], F32)]
        wo_hi = at("wo_hi", 67, [P, KC, D], F32R)
        wo_lo = at("wo_lo", 75, [P, KC, D], F32R)
        wo_raw = at("wo_raw", 75, [P, KC, D], F32)
        xT_raw = at("xT_raw", 83, [P, KC, T], F32)
        w_raw = at("w_raw", 99, [P, KC, 6 * P], F32)
        q_stack = [at(f"q_stack{b}", 83 + 8 * b, [P, REP * T], BF16) for b in range(3)]
        x1T_hi = at("x1T_hi", 83, [P, KC, T], F32R)
        x1T_lo = at("x1T_lo", 99, [P, KC, T], F32R)
        E = 115
        us = [at("u_a", 50, [P, UNIT], BF16), at("u_b", E + 88, [P, UNIT], BF16)]
        lines = [at("lines_a", 51, [P, 8, UNIT], F32), at("lines_b", E + 72, [P, 8, UNIT], F32)]
        w_hi = at("w_hi", E, [P, KC, 6 * P], F32R)
        w_lo = at("w_lo", E + 12, [P, KC, 6 * P], F32R)
        probs = at("probs", E, [P, 4, 2, HALF], F32)
        ctx_raw = at("ctx_raw", E + 24, [P, NH, HALF], F32)
        ctx_in = at("ctx_in", E + 28, [P, T], F32)
        rsum_in = at("rsum_in", E + 32, [P, T], F32)
        qk_parts = at("qk_parts", E + 24, [P, 4, 3, HALF], BF16)
        resid = at("resid", E + 51, [P, 2, HALF], F32)
        v_all = at("v_all", E + 36, [P, TT, P], F32)
        v_ones = [at(f"v_ones{b}", E + 40 + b, [P, TT, 32], F32) for b in range(3)]
        k_stack = [at(f"k_stack{b}", E + 43 + 2 * b, [P, T], BF16) for b in range(3)]
        neg_max = at("neg_max", E + 49, [32, 3, P], BF16)
        neg_max_f = at("neg_max_f", E + 49.75, [32, P], F32)
        sums = at("sums", E + 50.25, [P, T // HD], F32)
        xT_hi = at("xT_hi", E + 56, [P, KC, T], F32R)
        xT_lo = at("xT_lo", E + 72, [P, KC, T], F32R)
        ctx_hi = at("ctx_hi", E + 56, [P, KC, T], F32R)
        ctx_lo = at("ctx_lo", E + 72, [P, KC, T], F32R)
        bo_all = at("bo_all", 204, [P, D], F32)
        gu_hi = at("gu_hi", E, [P, 2, 2 * UNIT], F32R)
        gu_lo = at("gu_lo", E + 8, [P, 2, 2 * UNIT], F32R)
        hid = at("hid", E + 16, [P, MT, T], F32)
        wd_hi = at("wd_hi", 46, [P, MT, D], F32R)
        WD_EARLY = 4
        wd_lo_early = at("wd_lo_early", 74, [P, WD_EARLY, D], F32R)
        wd_lo_rest = at("wd_lo_rest", 83, [P, MT - WD_EARLY, D], F32R)
        hid_hi = [at("hid_hi0", E + 72, [P, MT, P], F32R), at("hid_hi1", E, [P, MT, P], F32R)]
        hid_lo = [at("hid_lo0", E + 79, [P, MT, P], F32R), at("hid_lo1", E + 7, [P, MT, P], F32R)]

        def wd_lo(j):
            return wd_lo_early[:, j, :] if j < WD_EARLY else wd_lo_rest[:, j - WD_EARLY, :]

        ps = nc.alloc_psum_tensor("ps", [P, 8, HALF], F32)
        B_MAX, B_CTX = (4, 5, 7), 6
        maxima_T = ps[0:32, B_MAX[2], 0:P]

        def sem(name):
            return ctx.enter_context(nc.semaphore(name))

        def sems(*names):
            return [sem(n) for n in names]

        xT_in = [sem(f"xT_in{k}") for k in range(KC)]
        w_in = [sem(f"w_in{k}") for k in range(KC)]
        xres_in, bo_in, wo_in, consts, k_ones = sems("xres_in", "bo_in", "wo_in", "consts", "k_ones")
        x_hi_s, x_lo_s, w_hi_s, w_lo_s, wo_hi_s, wo_lo_s = sems("x_hi_s", "x_lo_s", "w_hi_s", "w_lo_s", "wo_hi_s", "wo_lo_s")
        bo_added, proj, v_proj, v_ready, v_staged = sems("bo_added", "proj", "v_proj", "v_ready", "v_staged")
        part_h, part_r, part_m, parts = sems("part_h", "part_r", "part_m", "parts")
        parts_stored = [sem(f"parts_stored{b}") for b in range(4)]
        stack_in = [sem(f"stack_in{b}") for b in range(3)]
        max_scores, max_done, max_all, max_T = sems("max_scores", "max_done", "max_all", "max_T")
        nm_h, nm_r, nm_m, nm_all, mrow_in = sems("nm_h", "nm_r", "nm_m", "nm_all", "mrow_in")
        st_ready, exp_done, pv_done, ctx_evac = sems("st_ready", "exp_done", "pv_done", "ctx_evac")
        ctx_stored = [sem(f"ctx_stored{h}") for h in range(NH)]
        sums_in, sums_inv, rsum_stored, rsum_loaded, ctx_loaded = sems("sums_in", "sums_inv", "rsum_stored", "rsum_loaded", "ctx_loaded")
        ctx_mul, ctx_hi_s, ctx_lo_s = sems("ctx_mul", "ctx_hi_s", "ctx_lo_s")
        codes_in = [sem(f"codes_in{b}") for b in range(2)]
        scales_in = [sem(f"scales_in{b}") for b in range(2)]
        u_ready, line_ready, right_sum, left_pool, left_dve = sems("u_ready", "line_ready", "right_sum", "left_pool", "left_dve")
        dq_l0, dq_code, dq_w = sems("dq_l0", "dq_code", "dq_w")
        gu_hi_s, gu_lo_s = sems("gu_hi_s", "gu_lo_s")
        attn_out, ln_y, ln_st, ln_ag, ln_sd, ln_rs, ln_b, ln_x = sems(
            "attn_out", "ln_y", "ln_st", "ln_ag", "ln_sd", "ln_rs", "ln_b", "ln_x")
        x1T_ps, x1T_hi_s, x1T_lo_s = sems("x1T_ps", "x1T_hi_s", "x1T_lo_s")
        gate_up, silu_s, hid_s = sems("gate_up", "silu_s", "hid_s")
        wd_hi_s, wd_lo_s, hh_first, hl_first, hh_s, hl_s, down, out_s = sems(
            "wd_hi_s", "wd_lo_s", "hh_first", "hl_first", "hh_s", "hl_s", "down", "out_s")

        block = ctx.enter_context(nc.Block())

        KQ = [("k", 0, 0), ("k", 0, 1)] + [("q", mt, hf) for mt in range(KC) for hf in range(NH)]
        NKQ = len(KQ)
        EARLY_FROM, EARLY_MAX = 6, 6

        def unit_slot(n):
            if isinstance(n, int) and n >= MT:
                return hid[:, (n - MT) // 2, (n - MT) % 2 * UNIT:((n - MT) % 2 + 1) * UNIT]
            return w_down[:, bass.ds(n, 1), :].rearrange("p a n -> p (a n)")

        def window_slot(j, which):
            return hid[:, bass.ds(j + (ATTN_UNITS - MT) // 2, 1), which * UNIT:(which + 1) * UNIT].rearrange(
                "p a n -> p (a n)")

        @block.sync
        def _(sp):
            def load_codes(n, buf=0, step=1):
                if step:
                    sp.wait_ge(u_ready, n - step + 1)
                sp.dma_start(codes[buf][:], t["codes"][bass.ds(n, 1), :, :].rearrange("a p n -> (a p) n")).then_inc(codes_in[buf], 16)

            def load_scales(n, buf=0, step=1):
                if step:
                    sp.wait_ge(dq_w, n - step + 1)
                sp.dma_start(scales[buf][:], t["scales"][bass.ds(n, 1), :, :].rearrange("a b n -> (a b) n").unsqueeze(1)
                             .to_broadcast([2, BLOCK, UNIT])).then_inc(scales_in[buf], 16)

            def load_queries(buf, g):
                for blk, part in enumerate(Q_PART):
                    sp.dma_start(q_stack[buf][HD * blk:HD * (blk + 1), :],
                                 t["q_scr"][part, bass.ds(g * REP * HD, REP * HD), :].rearrange(
                                     "(d r) t -> d (r t)", r=REP)).then_inc(stack_in[buf], 16)

            def load_keys(buf, g):
                for blk, part in enumerate(K_PART):
                    sp.dma_start(k_stack[buf][HD * blk:HD * (blk + 1), :],
                                 t["k_scr"][part, bass.ds(g * HD, HD), :]).then_inc(stack_in[buf], 16)

            def mrows(buf, g):
                sp.wait_ge(nm_all, g + 1)
                for c in range(3):
                    sp.dma_start(q_stack[buf][MROW + c:MROW + c + 1, :].rearrange("a (n q) -> a n q", q=P),
                                 neg_max[:, c, :]).then_inc(mrow_in, 16)

            def store_ctx(g, hf):
                sp.wait_ge(ctx_evac, NH * g + hf + 1 + FREE)
                sp.dma_start(t["ctx_scr"][bass.ds(g, 1), :, hf * HALF:(hf + 1) * HALF].rearrange("a p n -> (a p) n"),
                             ctx_raw[:, hf, :]).then_inc(ctx_stored[hf], 16)

            scr = t["ctx_scr"].rearrange("g (r two d) n -> (g r) two d n", two=2, d=HD)

            def load_ctx(ch):
                for hf in range(NH):
                    sp.wait_ge(ctx_stored[hf], 16 * (2 * (ch + 1) + FREE))
                heads = slice(2 * REP * ch, 2 * REP * (ch + 1))
                if ch:
                    sp.wait_ge(rsum_stored, 16 * ch)
                sp.dma_start(sums[:], scr[heads, 1, 0, :].rearrange("h (a b) -> h a b", a=HD)).then_inc(sums_in, 16)
                if ch:
                    sp.wait_ge(ctx_mul, ch)
                sp.dma_start(ctx_in[:], scr[heads, 0, :, :]).then_inc(ctx_loaded, 16)
                sp.wait_ge(sums_inv, ch + 1)
                sp.dma_start(t["rsum_scr"][ch, :, :].rearrange("h (a b) -> h a b", a=HD), sums[:]).then_inc(rsum_stored, 16)
                sp.wait_ge(rsum_stored, 16 * (ch + 1))
                if ch:
                    sp.wait_ge(ctx_lo_s, ch)
                sp.dma_start(rsum_in[:], t["rsum_scr"][ch, :, :].unsqueeze(1).to_broadcast([2 * REP, HD, T])).then_inc(rsum_loaded, 16)

            for kc in range(KC):
                sp.dma_start(xT_raw[:, kc, :], t["xT"][kc * P:(kc + 1) * P, :]).then_inc(xT_in[kc], 16)
                sp.dma_start(w_raw[:, kc, :], t["w_qkv"][kc * P:(kc + 1) * P, :]).then_inc(w_in[kc], 16)
            load_codes(0, step=0)
            load_scales(0, step=0)
            sp.dma_start(wo_raw[:], t["wo"].rearrange("(c p) n -> p c n", p=P)).then_inc(wo_in, 16)
            for e, (which, mt, hf) in enumerate(KQ):
                sp.wait_ge(parts, e + 1)
                dst = t["k_scr"] if which == "k" else t["q_scr"]
                sp.dma_start(dst[:, mt * P:(mt + 1) * P, hf * HALF:(hf + 1) * HALF].rearrange("c p t -> p c t"),
                             qk_parts[:, e % 4, :, :]).then_inc(parts_stored[e % 4], 16)
                if e == 2:
                    for b in range(2):
                        sp.wait_ge(parts_stored[b], 16)
                    load_keys(0, 0)
                if e == 3:
                    for b in range(2, 4):
                        sp.wait_ge(parts_stored[b], 16)
                    sp.wait_ge(x_lo_s, KC)
                    sp.wait_ge(w_lo_s, KC)
                    load_queries(0, 0)
                if e == 5:
                    load_codes(1)
                    load_keys(1, 1)
                if e == 7:
                    load_queries(1, 1)
                    load_scales(1)
            load_codes(2)
            for b in range(4):
                sp.wait_ge(parts_stored[b], 16 * ((NKQ - b + 3) // 4))
            load_scales(2)
            load_codes(3)
            mrows(0, 0)
            load_scales(3)
            load_codes(4)
            sp.dma_start(xres[:], t["x"].rearrange("(n p) d -> p n d", p=P)).then_inc(xres_in, 16)
            sp.dma_start(bo_all[:], t["bo"].rearrange("(a n) -> a n", a=1).to_broadcast([P, D])).then_inc(bo_in, 16)

            def group(g, c, n, units):
                sp.wait_ge(st_ready, NST * g + 1)
                load_queries((c + 2) % 3, g + 2)
                load_keys((c + 2) % 3, g + 2)
                load_scales(n)
                load_codes(n + 1)
                store_ctx(g, 0)
                if units == 2:
                    load_scales(n + 1)
                    load_codes(n + 2)
                mrows((c + 1) % 3, g + 1)
                store_ctx(g, 1)

            with sp.Fori(0, 2) as it:
                for c in range(3):
                    group(it * 3 + c, c, it * sum(LOOP_UNITS) + EARLY_UNITS + sum(LOOP_UNITS[:c]), LOOP_UNITS[c])
            n = LATE
            load_ctx(0)
            load_scales(n)
            load_codes(n + 1)
            store_ctx(6, 0)
            load_scales(n + 1)
            load_codes(n + 2)
            mrows(1, 7)
            load_ctx(1)
            store_ctx(6, 1)
            load_scales(n + 2)
            load_ctx(2)
            load_codes(n + 3)
            store_ctx(7, 0)
            load_scales(n + 3)
            load_codes(n + 4)
            store_ctx(7, 1)
            load_ctx(3)
            load_scales(n + 4)
            load_codes(n + 5)
            load_scales(n + 5)
            load_codes(n + 6)
            sp.wait_ge(attn_out, TT)
            load_codes(n + 7, 1, step=0)
            load_scales(n + 7, 1, step=0)
            load_scales(n + 6)
            with sp.Fori(0, NW - 1) as j:
                for which in range(2):
                    load_codes(2 * j + ATTN_UNITS + 2 + which, which, step=2)
                    load_scales(2 * j + ATTN_UNITS + 2 + which, which, step=2)
            with sp.Fori(0, TT) as tt:
                sp.wait_ge(ln_x, TT + tt + 1)
                sp.dma_start(t["out"][bass.ds(tt * P, P), :],
                             xres[:, bass.ds(tt, 1), :].rearrange("p a d -> p (a d)")).then_inc(out_s, 16)
            sp.wait_ge(out_s, 16 * TT)

        @block.gpsimd
        def _(pool):
            for m in (ident_f, ident_b, mask_q, mask_k):
                pool.memset(m[:], 0.0).then_inc(consts, 1)
            pool.memset(eps[:], EPS).then_inc(consts, 1)
            for b in range(3):
                pool.memset(v_ones[b][:, :, HD:32], 1.0).then_inc(consts, 1)
            pool.wait_ge(consts, 4)
            for m, op, fill, sign in ((ident_f, ALU.not_equal, 1.0, 1), (ident_b, ALU.not_equal, 1.0, 1),
                                      (mask_q, ALU.is_ge, NEG, 1), (mask_k, ALU.is_ge, NEG, -1)):
                pool.affine_select(out=m[:], in_=m[:], compare_op=op, fill=fill, base=0,
                                   pattern=[[-sign, P]], channel_multiplier=sign).then_inc(consts, 1)
            N_CONSTS = 12

            def right_add(n, i, buf=0):
                pool.wait_ge(line_ready, n * NLINE + i + 2)
                if i:
                    pool.wait_ge(right_sum, n * 3 + i)
                pool.tensor_tensor(lines[buf][:, R0, :], lines[buf][:, R0, :], lines[buf][:, R1 + i, :],
                                   ALU.add).then_inc(right_sum, 1)

            def weight(n, out, buf, k):
                pool.wait_ge(dq_code, n + 1)
                pool.wait_ge(scales_in[buf], 16 * (k + 1))
                pool.tensor_tensor(out, lines[buf][:, L0, :], scales[buf][:], ALU.mult).then_inc(dq_w, 1)

            def unit(n, out):
                L = lines[0]
                for i in range(3):
                    right_add(n, i)
                pool.wait_ge(dq_l0, n + 1)
                for i, src in enumerate((L1, L2, L3)):
                    pool.wait_ge(line_ready, n * NLINE + i + 5)
                    if i:
                        pool.wait_ge(left_pool, n * 3 + i)
                    pool.tensor_tensor(L[:, L0, :], L[:, L0, :], L[:, src, :], ALU.add).then_inc(left_pool, 1)
                pool.wait_ge(right_sum, n * 3 + 3)
                pool.wait_ge(left_pool, n * 3 + 3)
                pool.tensor_tensor(L[:, L0, :], L[:, R0, :], L[:, L0, :], ALU.subtract).then_inc(dq_code, 1)
                weight(n, out, 0, n)

            def stage_v(buf, g):
                pool.tensor_copy(v_ones[buf][:, :, 0:HD], v_all[:, :, bass.ds(g * HD, HD)]).then_inc(v_staged, 1)

            for n in range(EARLY_UNITS - 1):
                unit(n, unit_slot(n))
            pool.wait_ge(v_ready, 2)
            pool.wait_ge(consts, N_CONSTS)
            stage_v(0, 0)
            unit(EARLY_UNITS - 1, unit_slot(EARLY_UNITS - 1))

            def group(g, c, n, count):
                pool.wait_ge(pv_done, NPV * g + 1)
                stage_v((c + 1) % 3, g + 1)
                for k in range(count):
                    unit(n + k, unit_slot(n + k))

            with pool.Fori(0, 2) as it:
                for c in range(3):
                    group(it * 3 + c, c, it * sum(LOOP_UNITS) + EARLY_UNITS + sum(LOOP_UNITS[:c]), LOOP_UNITS[c])
            group(6, 0, LATE, 2)
            for n in range(LATE + 2, ATTN_UNITS):
                if n == LATE + 4:
                    for hf in range(NH):
                        pool.wait_ge(ctx_stored[hf], 16 * (G + FREE))
                unit(n, unit_slot(n))
            pool.wait_ge(attn_out, TT)
            with pool.Fori(0, NW) as j:
                n = 2 * j + ATTN_UNITS
                for i in range(3):
                    right_add(n, i, 0)
                right_add(n + 1, 0, 1)
                weight(n, window_slot(j, 0), 0, j + ATTN_UNITS)
                for i in range(1, 3):
                    right_add(n + 1, i, 1)
                weight(n + 1, window_slot(j, 1), 1, j)

        @block.scalar
        def _(act):
            def line_pass(n, k, buf=0, prev=1):
                if k == 0:
                    act.wait_ge(u_ready, n + 1)
                    if prev:
                        act.wait_ge(dq_w, n + 1 - prev)
                a, b = LINES[k]
                act.activation(lines[buf][:, k, :], us[buf][:], ACT.Relu, bias=b, scale=a).then_inc(line_ready, 1)

            def unit(n, buf=0, prev=1):
                for k in range(NLINE):
                    line_pass(n, k, buf, prev)

            act.sem_inc(ctx_evac, FREE)
            for hf in range(NH):
                act.sem_inc(ctx_stored[hf], 16 * FREE)
            for kc in range(KC):
                act.wait_ge(xT_in[kc], 16)
                act.activation(xT_hi[:, kc, :], xT_raw[:, kc, :], ACT.Copy).then_inc(x_hi_s, 1)
                act.wait_ge(w_in[kc], 16)
                act.activation(w_hi[:, kc, :], w_raw[:, kc, :], ACT.Copy).then_inc(w_hi_s, 1)

            def high_part(e):
                act.wait_ge(proj, e + 1)
                if e >= 4:
                    act.wait_ge(parts_stored[e % 4], 16 * (e // 4))
                act.activation(qk_parts[:, e % 4, 0, :], ps[:, e % 4, :], ACT.Copy).then_inc(part_h, 1)

            def middle_part(e):
                act.wait_ge(part_r, e + 1)
                act.activation(qk_parts[:, e % 4, 1, :], resid[:, e % 2, :], ACT.Copy).then_inc(part_m, 1)

            for e in range(NKQ):
                high_part(e)
                if e not in (0, 4, 6):
                    middle_part(e - 1)
                if e in (3, 5, NKQ - 1):
                    middle_part(e)
                if e == 3:
                    unit(0, prev=0)
                if e == 5:
                    for hf in range(NH):
                        act.wait_ge(v_proj, hf + 1)
                        act.activation(v_all[:, 4 * hf:4 * hf + 4, :], ps[:, 6 + hf, :], ACT.Copy).then_inc(v_ready, 1)
                if e == 8:
                    unit(1)
            unit(2)
            act.wait_ge(wo_in, 16)
            act.activation(wo_hi[:], wo_raw[:], ACT.Copy).then_inc(wo_hi_s, 1)
            unit(3)

            def evac(g, hf):
                act.wait_ge(pv_done, NPV * g + (4 if hf == 0 else NPV))
                act.wait_ge(ctx_stored[hf], 16 * (g + FREE))
                act.activation(ctx_raw[:, hf, :], ps[:, B_CTX, :], ACT.Copy).then_inc(ctx_evac, 1)

            def split_ctx(ch):
                act.wait_ge(ctx_mul, ch + 1)
                act.activation(ctx_hi[:, ch, :], rsum_in[:], ACT.Copy).then_inc(ctx_hi_s, 1)

            def group(g, n, count, chunks=()):
                at_step = [5 + i for i in range(NLINE)] + [17 + i for i in range(NLINE)]
                for s, (qh, kt, pr) in enumerate(STEPS):
                    w = (qh + 1) * HALF - q_from(qh, kt)
                    act.wait_ge(st_ready, NST * g + s + 1)
                    if s >= 4:
                        act.wait_ge(pv_done, NPV * g + (s - 4) // 2 + 1)
                    act.activation(probs[:, s % 4, :, 0:w], ps[:, 2 * (s % 2):2 * (s % 2) + 2, 0:w], ACT.Exp,
                                   scale=SCALE).then_inc(exp_done, 1)
                    if s == 9:
                        evac(g, 0)
                    if s in at_step and at_step.index(s) < NLINE * count:
                        k = at_step.index(s)
                        line_pass(n + k // NLINE, k % NLINE)
                    for ch, step in chunks:
                        if s == step:
                            split_ctx(ch)
                evac(g, 1)

            with act.Fori(0, 2) as it:
                for c in range(3):
                    group(it * 3 + c, it * sum(LOOP_UNITS) + EARLY_UNITS + sum(LOOP_UNITS[:c]), LOOP_UNITS[c])
            group(6, LATE, 2, chunks=((0, 12),))
            group(7, LATE + 2, 2, chunks=((1, 4), (2, 16)))
            unit(LATE + 4)
            split_ctx(3)

            def std(n, slot):
                act.wait_ge(ln_ag, n + 1)
                act.activation(ln_std[:, slot, :], ln_mv[:, slot, 1:2], ACT.Sqrt, bias=eps[:]).then_inc(ln_sd, 1)

            def normalise(n, tt, slot):
                act.wait_ge(ln_b, n + 1)
                x_tt = xres[:, bass.ds(tt, 1), :].rearrange("p a d -> p (a d)")
                act.activation(x_tt, x_tt, ACT.Identity, bias=ln_nb[:, slot, :], scale=ln_rstd[:, slot, :]).then_inc(ln_x, 1)

            for tt in range(TT + 2):
                if tt < TT:
                    std(tt, tt % 4)
                if 1 <= tt <= TT:
                    normalise(tt - 1, tt - 1, (tt - 1) % 4)
                    if tt <= NLINE:
                        line_pass(LATE + 5, tt - 1)
                if tt >= 2:
                    act.wait_ge(x1T_ps, tt - 1)
                    act.activation(x1T_hi[:, :, (tt - 2) * P:(tt - 1) * P],
                                   ps[:, tt - 2, :].rearrange("p (c n) -> p c n", c=KC), ACT.Copy).then_inc(x1T_hi_s, 1)

            def silu(j, par):
                act.wait_ge(gate_up, 2 * j + 1)
                act.activation(hid[:, bass.ds(j, 1), :].rearrange("p a n -> p (a n)"),
                               ps[:, 4 * par:4 * par + 2, :].rearrange("p a n -> p (a n)"), ACT.Silu).then_inc(silu_s, 1)

            def window(j, par, first=False):
                n = 2 * j + ATTN_UNITS
                if first:
                    unit(n)
                act.wait_ge(gu_lo_s, j + 1)
                silu(j, par)
                if not first:
                    unit(n, 0, 2)
                unit(n + 1, 1, 0 if first else 2)

            window(0, 0, first=True)
            with act.Fori(1, NW - 3, 2) as j:
                window(j, 1)
                window(j + 1, 0)
            window(NW - 2, 1)
            window(NW - 1, 0)
            for j in range(NW, MT):
                act.wait_ge(gu_lo_s, j + 1)
                silu(j, j % 2)
                if j == NW:
                    act.wait_ge(dq_w, UNITS)
                half = MT // 2 * (j - NW)
                for i in range(half, min(half + MT // 2, MT)):
                    act.activation(wd_hi[:, i, :], w_down[:, i, :], ACT.Copy).then_inc(wd_hi_s, 1)
                if j == MT - 2:
                    act.wait_ge(hid_s, MT - 1)
                    act.activation(hid_hi[0][:, 0:MT - 1, :], hid[:, 0:MT - 1, 0:P], ACT.Copy).then_inc(hh_first, 1)

            def split_hidden(tt, par):
                act.activation(hid_hi[par][:], hid[:, :, bass.ds(tt * P, P)], ACT.Copy).then_inc(hh_s, 1)

            def out_tile(tt, par, more=True):
                if more:
                    act.wait_ge(down, tt + 1)
                    split_hidden(tt + 2, par)
                std(tt + TT, par)
                normalise(tt + TT, tt, par)

            act.wait_ge(hid_s, MT)
            act.activation(hid_hi[0][:, MT - 1, :], hid[:, MT - 1, 0:P], ACT.Copy).then_inc(hh_s, 1)
            split_hidden(1, 1)
            with act.Fori(0, TT - 3, 2) as tt:
                for par in range(2):
                    out_tile(tt + par, par)
            for par in range(2):
                out_tile(TT - 2 + par, par, more=False)

        @block.vector
        def _(dve):
            def u_of(n, buf, k, prev):
                dve.wait_ge(codes_in[buf], 16 * (k + 1))
                if prev:
                    dve.wait_ge(line_ready, (n + 1 - prev) * NLINE)
                    dve.wait_ge(dq_l0, n + 1 - prev)
                dve.tensor_scalar(us[buf][:], codes[buf][:], float(-ZERO_AT), None, ALU.add).then_inc(u_ready, 1)

            def first_left(n, buf, prev):
                dve.wait_ge(u_ready, n + 1)
                if prev:
                    dve.wait_ge(dq_w, n + 1 - prev)
                dve.tensor_scalar(lines[buf][:, L0, :], us[buf][:], SLOPE_L0, 0.0, ALU.mult, ALU.max).then_inc(dq_l0, 1)

            def make_u(n, prev=1):
                u_of(n, 0, n, prev)
                first_left(n, 0, prev)

            for b in range(3):
                dve.memset(k_stack[b][MROW:STACKM, :], 1.0).then_inc(k_ones, 1)
            for kc in range(KC):
                dve.wait_ge(x_hi_s, kc + 1)
                dve.tensor_tensor(xT_lo[:, kc, :], xT_raw[:, kc, :], xT_hi[:, kc, :].bitcast(F32), ALU.subtract).then_inc(x_lo_s, 1)
                dve.wait_ge(w_hi_s, kc + 1)
                dve.tensor_tensor(w_lo[:, kc, :], w_raw[:, kc, :], w_hi[:, kc, :].bitcast(F32), ALU.subtract).then_inc(w_lo_s, 1)
            make_u(0, prev=0)

            def residual(e):
                dve.wait_ge(part_h, e + 1)
                if e >= 2:
                    dve.wait_ge(parts, e - 1)
                dve.tensor_tensor(resid[:, e % 2, :], ps[:, e % 4, :], qk_parts[:, e % 4, 0, :], ALU.subtract).then_inc(part_r, 1)

            def low_part(e):
                dve.wait_ge(part_m, e + 1)
                dve.tensor_tensor(qk_parts[:, e % 4, 2, :], resid[:, e % 2, :], qk_parts[:, e % 4, 1, :],
                                  ALU.subtract).then_inc(parts, 1)

            def reduce(idx, k, buf):
                i, kh, r = MAX_TILES[k]
                n = width(i, kh)
                dve.wait_ge(max_scores, idx + 1)
                dst = row_max[:, buf, r * TT + i:r * TT + i + 1] if kh == 0 else row_max_hi[:, r, i - 4:i - 3]
                dve.reduce_max(dst, ps[:, B_MAX[k % 3], 0:n], AX.X).then_inc(max_done, 1)

            def combine(g, buf):
                dve.wait_ge(max_done, NMAX * g + NMAX)
                v = row_max[:, buf, :].rearrange("p (r i) -> p r i", r=REP)[:, :, 4:8]
                dve.tensor_tensor(v, v, row_max_hi[:], ALU.max).then_inc(max_all, 1)

            def negate(g, first=False):
                dve.wait_ge(max_T, g + 1)
                if not first:
                    dve.wait_ge(mrow_in, 48 * g)
                dve.tensor_scalar(neg_max[:, 0, :], maxima_T, -1.0, None, ALU.mult).then_inc(nm_h, 1)
                dve.wait_ge(nm_h, g + 1)
                dve.scalar_tensor_tensor(neg_max_f[:], maxima_T, -1.0, neg_max[:, 0, :], ALU.mult, ALU.subtract).then_inc(nm_r, 1)
                dve.wait_ge(nm_r, g + 1)
                dve.tensor_copy(neg_max[:, 1, :], neg_max_f[:]).then_inc(nm_m, 1)
                dve.wait_ge(nm_m, g + 1)
                dve.tensor_tensor(neg_max[:, 2, :], neg_max_f[:], neg_max[:, 1, :], ALU.subtract).then_inc(nm_all, 1)

            early = 0
            for e in range(NKQ):
                if e >= EARLY_FROM:
                    for _ in range(EARLY_MAX):
                        reduce(early, early, 0)
                        early += 1
                residual(e)
                if e not in (0, 4, 6):
                    low_part(e - 1)
                if e in (3, 5, NKQ - 1):
                    low_part(e)
                if e == 7:
                    make_u(1)
            for k in range(early, NMAX):
                reduce(k, k, 0)
                if k == early + 9:
                    make_u(2)
            combine(0, 0)
            negate(0, first=True)
            for k in range(LEAD):
                reduce(NMAX + k, k, 1)
            make_u(3)

            def invert_sums(ch):
                dve.wait_ge(sums_in, 16 * (ch + 1))
                dve.reciprocal(sums[:], sums[:]).then_inc(sums_inv, 1)

            def scale_ctx(ch):
                dve.wait_ge(ctx_loaded, 16 * (ch + 1))
                dve.wait_ge(rsum_loaded, 16 * (ch + 1))
                dve.tensor_tensor(rsum_in[:], ctx_in[:], rsum_in[:], ALU.mult).then_inc(ctx_mul, 1)

            def ctx_low(ch):
                dve.wait_ge(ctx_hi_s, ch + 1)
                dve.tensor_tensor(ctx_lo[:, ch, :], rsum_in[:], ctx_hi[:, ch, :].bitcast(F32), ALU.subtract).then_inc(ctx_lo_s, 1)

            def group(g, c, n, units, count=NMAX, before={}):
                for s in range(count):
                    k = (LEAD + s) % NMAX
                    if s in before:
                        before[s]()
                    if s == 9:
                        make_u(n)
                    if s == 31 and units == 2:
                        make_u(n + 1)
                    if s == 0:
                        dve.wait_ge(max_all, g + 1)
                    reduce(NMAX * (g + 1) + LEAD + s, k, (c + 1 + (LEAD + s) // NMAX) % 3)
                    if s == NMAX - LEAD - 1:
                        combine(g + 1, (c + 1) % 3)
                    if s == NMAX - LEAD + 1:
                        negate(g + 1)
                if count == NMAX - LEAD:
                    negate(g + 1)

            with dve.Fori(0, 2) as it:
                for c in range(3):
                    group(it * 3 + c, c, it * sum(LOOP_UNITS) + EARLY_UNITS + sum(LOOP_UNITS[:c]), LOOP_UNITS[c])
            group(6, 0, LATE, 2, count=NMAX - LEAD, before={
                8: lambda: invert_sums(0), 20: lambda: scale_ctx(0), 26: lambda: ctx_low(0)})
            invert_sums(1)
            make_u(LATE + 2)
            scale_ctx(1)
            dve.wait_ge(xres_in, 16)
            dve.wait_ge(bo_in, 16)
            dve.tensor_tensor(xres[:], xres[:], bo_all[:].unsqueeze(1).to_broadcast([P, TT, D]), ALU.add).then_inc(bo_added, 1)
            ctx_low(1)
            dve.wait_ge(wo_hi_s, 1)
            dve.tensor_tensor(wo_lo[:], wo_raw[:], wo_hi[:].bitcast(F32), ALU.subtract).then_inc(wo_lo_s, 1)
            invert_sums(2)
            scale_ctx(2)
            ctx_low(2)
            make_u(LATE + 3)

            def slot_of(j):
                return hid[:, bass.ds(j, 1), :].rearrange("p a n -> p (a n)")

            def weights_high(j, par):
                dve.wait_ge(dq_w, 2 * j + MT + 2)
                dve.tensor_copy(gu_hi[:, par, :], slot_of(j)).then_inc(gu_hi_s, 1)

            def weights_low(j, par):
                dve.wait_ge(gu_hi_s, j + 1)
                dve.tensor_tensor(gu_lo[:, par, :], slot_of(j), gu_hi[:, par, :].bitcast(F32), ALU.subtract).then_inc(gu_lo_s, 1)

            def split_gate_up(j, par):
                weights_high(j, par)
                weights_low(j, par)

            dve.wait_ge(pv_done, NPV * G)
            split_gate_up(0, 0)
            invert_sums(3)
            split_gate_up(1, 1)
            make_u(LATE + 4)
            scale_ctx(3)
            ctx_low(3)

            def x_tile(tt):
                return xres[:, bass.ds(tt, 1), :].rearrange("p a d -> p (a d)")

            def ln_sum(n, tt, src):
                dve.tensor_tensor(x_tile(tt), src, x_tile(tt), ALU.add).then_inc(ln_y, 1)

            def ln_statistics(n, tt, slot):
                dve.wait_ge(ln_y, n + 1)
                dve.bn_stats(ln_stats[:, slot % 2, :], x_tile(tt)).then_inc(ln_st, 1)

            def ln_variance(n, slot):
                dve.wait_ge(ln_st, n + 1)
                dve.bn_aggr(ln_mv[:, slot, :], ln_stats[:, slot % 2, :]).then_inc(ln_ag, 1)

            def ln_inverse(n, slot):
                dve.wait_ge(ln_sd, n + 1)
                dve.reciprocal(ln_rstd[:, slot, :], ln_std[:, slot, :]).then_inc(ln_rs, 1)

            def ln_bias(n, slot):
                dve.wait_ge(ln_rs, n + 1)
                dve.scalar_tensor_tensor(ln_nb[:, slot, :], ln_mv[:, slot, 0:1], -1.0, ln_rstd[:, slot, :],
                                         ALU.mult, ALU.mult).then_inc(ln_b, 1)

            dve.wait_ge(bo_added, 1)
            for tt in range(TT + 3):
                if tt < TT:
                    dve.wait_ge(attn_out, tt + 1)
                    ln_sum(tt, tt, ps[:, tt, :])
                if 1 <= tt <= TT:
                    ln_inverse(tt - 1, (tt - 1) % 4)
                if tt < TT:
                    if tt >= 4:
                        dve.wait_ge(ln_x, tt - 3)
                    ln_statistics(tt, tt, tt % 4)
                if 1 <= tt <= TT:
                    ln_bias(tt - 1, (tt - 1) % 4)
                if tt < TT:
                    ln_variance(tt, tt % 4)
                if tt == 0:
                    make_u(LATE + 5)
                if tt >= 3:
                    dve.wait_ge(x1T_hi_s, tt - 2)
                    dve.tensor_tensor(x1T_lo[:, :, (tt - 3) * P:(tt - 2) * P],
                                      ps[:, tt - 3, :].rearrange("p (c n) -> p c n", c=KC),
                                      x1T_hi[:, :, (tt - 3) * P:(tt - 2) * P].bitcast(F32), ALU.subtract).then_inc(x1T_lo_s, 1)

            def hidden_product(j, par):
                dve.wait_ge(gate_up, 2 * j + 2)
                dve.wait_ge(silu_s, j + 1)
                slot = hid[:, bass.ds(j, 1), :].rearrange("p a n -> p (a n)")
                dve.tensor_tensor(slot, slot, ps[:, 4 * par + 2:4 * par + 4, :].rearrange("p a n -> p (a n)"),
                                  ALU.mult).then_inc(hid_s, 1)

            def left_sum(n, buf, i, done):
                dve.wait_ge(line_ready, n * NLINE + i + 5)
                if i:
                    dve.wait_ge(left_dve, done + i)
                else:
                    dve.wait_ge(dq_l0, n + 1)
                dve.tensor_tensor(lines[buf][:, L0, :], lines[buf][:, L0, :], lines[buf][:, L1 + i, :],
                                  ALU.add).then_inc(left_dve, 1)

            def code_of(n, buf, done):
                dve.wait_ge(left_dve, done + 3)
                dve.wait_ge(right_sum, n * 3 + 3)
                dve.tensor_tensor(lines[buf][:, L0, :], lines[buf][:, R0, :], lines[buf][:, L0, :],
                                  ALU.subtract).then_inc(dq_code, 1)

            def window(j, par, first=False, last=False):
                n = 2 * j + ATTN_UNITS
                if not first:
                    hidden_product(j, par)
                left_sum(n, 0, 0, 6 * j)
                if not first:
                    weights_high(j + 2, par)
                left_sum(n, 0, 1, 6 * j)
                if not first:
                    weights_low(j + 2, par)
                left_sum(n, 0, 2, 6 * j)
                first_left(n + 1, 1, 0 if first else 2)
                code_of(n, 0, 6 * j)
                if first:
                    hidden_product(j, par)
                    split_gate_up(j + 2, par)
                left_sum(n + 1, 1, 0, 6 * j + 3)
                if not last:
                    u_of(n + 2, 0, j + ATTN_UNITS + 1, 2)
                left_sum(n + 1, 1, 1, 6 * j + 3)
                left_sum(n + 1, 1, 2, 6 * j + 3)
                if not last:
                    first_left(n + 2, 0, 2)
                code_of(n + 1, 1, 6 * j + 3)
                if not last:
                    u_of(n + 3, 1, j + 1, 2)

            u_of(ATTN_UNITS, 0, ATTN_UNITS, 1)
            first_left(ATTN_UNITS, 0, 1)
            u_of(ATTN_UNITS + 1, 1, 0, 0)
            window(0, 0, first=True)
            with dve.Fori(1, NW - 3, 2) as j:
                window(j, 1)
                window(j + 1, 0)
            window(NW - 2, 1)
            window(NW - 1, 0, last=True)

            def down_low(j):
                dve.wait_ge(wd_hi_s, j + 1)
                dve.tensor_tensor(wd_lo(j), w_down[:, j, :], wd_hi[:, j, :].bitcast(F32), ALU.subtract).then_inc(wd_lo_s, 1)

            def hidden_low(tt, par):
                dve.wait_ge(hh_s, tt + 1)
                dve.tensor_tensor(hid_lo[par][:], hid[:, :, bass.ds(tt * P, P)], hid_hi[par][:].bitcast(F32),
                                  ALU.subtract).then_inc(hl_s, 1)

            hidden_product(NW, NW % 2)
            split_gate_up(NW + 2, NW % 2)
            for j in range(WD_EARLY):
                down_low(j)
            hidden_product(NW + 1, (NW + 1) % 2)
            dve.wait_ge(hh_first, 1)
            dve.tensor_tensor(hid_lo[0][:, 0:MT - 1, :], hid[:, 0:MT - 1, 0:P],
                              hid_hi[0][:, 0:MT - 1, :].bitcast(F32), ALU.subtract).then_inc(hl_first, 1)
            hidden_product(NW + 2, (NW + 2) % 2)
            for j in range(WD_EARLY, WD_EARLY + 2):
                down_low(j)
            dve.wait_ge(hh_s, 1)
            dve.tensor_tensor(hid_lo[0][:, MT - 1, :], hid[:, MT - 1, 0:P],
                              hid_hi[0][:, MT - 1, :].bitcast(F32), ALU.subtract).then_inc(hl_s, 1)
            for j in range(WD_EARLY + 2, MT):
                down_low(j)
            hidden_low(1, 1)

            def out_tile(tt, par, more=True):
                dve.wait_ge(down, tt + 1)
                dve.wait_ge(ln_x, tt + TT - 1)
                ln_sum(tt + TT, tt, ps[:, par, :])
                ln_statistics(tt + TT, tt, par)
                ln_variance(tt + TT, par)
                if more:
                    hidden_low(tt + 2, par)
                ln_inverse(tt + TT, par)
                ln_bias(tt + TT, par)

            for tt in range(TT):
                out_tile(tt, tt % 2, more=tt < TT - 2)

        @block.tensor
        def _(pe):
            def three_pass(out, a_hi, a_lo, b_hi, b_lo, chunks, start=True, stop=True):
                mm, n, at_ = None, 3 * len(chunks), 0
                for c in chunks:
                    for a, b in ((a_hi, b_hi), (a_hi, b_lo), (a_lo, b_hi)):
                        mm = pe.matmul(out, a(c), b(c), start=start and at_ == 0, stop=stop and at_ == n - 1)
                        at_ += 1
                return mm

            def max_tile(idx, k, buf, free=True):
                i, kh, r = MAX_TILES[k]
                n = width(i, kh)
                bank = B_MAX[k % 3]
                diag = n < HALF or (i + 1) * P == (kh + 1) * HALF
                if free:
                    pe.wait_ge(max_done, idx - 2)
                mm = pe.matmul(ps[:, bank, 0:n], q_stack[buf][0:STACK, r * T + i * P:r * T + (i + 1) * P],
                               k_stack[buf][0:STACK, kh * HALF:kh * HALF + n], start=True, stop=not diag)
                if diag:
                    mm = pe.matmul(ps[:, bank, n - P:n], ident_b[:], mask_q[:], start=False, stop=True)
                mm.then_inc(max_scores, 1)

            def project(e, chunks):
                which, mt, hf = KQ[e]
                col = 4 * P if which == "k" else mt * P
                return three_pass(ps[:, e % 4, :], lambda c: w_hi[:, c, col:col + P], lambda c: w_lo[:, c, col:col + P],
                                  lambda c: xT_hi[:, c, hf * HALF:(hf + 1) * HALF],
                                  lambda c: xT_lo[:, c, hf * HALF:(hf + 1) * HALF], chunks,
                                  start=chunks[0] == 0, stop=chunks[-1] == KC - 1)

            for kc in range(KC):
                pe.wait_ge(x_lo_s, kc + 1)
                pe.wait_ge(w_lo_s, kc + 1)
                for e in range(4):
                    mm = project(e, [kc])
                    if kc == KC - 1:
                        mm.then_inc(proj, 1)
            def project_v():
                for hf in range(NH):
                    for q4 in range(4):
                        tok = (4 * hf + q4) * P
                        mm = three_pass(ps[:, 6 + hf, q4 * P:(q4 + 1) * P], lambda c: xT_hi[:, c, tok:tok + P],
                                        lambda c: xT_lo[:, c, tok:tok + P], lambda c: w_hi[:, c, 5 * P:6 * P],
                                        lambda c: w_lo[:, c, 5 * P:6 * P], range(KC))
                    mm.then_inc(v_proj, 1)

            early = 0
            for e in range(4, NKQ):
                if e == 6:
                    project_v()
                pe.wait_ge(part_r, e - 3)
                if e < EARLY_FROM:
                    project(e, range(KC)).then_inc(proj, 1)
                    continue
                if e == EARLY_FROM:
                    pe.wait_ge(v_ready, NH)
                    pe.wait_ge(consts, 12)
                    pe.wait_ge(k_ones, 3)
                for half in range(2):
                    mm = project(e, range(2 * half, 2 * half + 2))
                    if half == 1:
                        mm.then_inc(proj, 1)
                    if e == EARLY_FROM and half == 0:
                        pe.wait_ge(stack_in[0], 192)
                    for _ in range(EARLY_MAX // 2):
                        max_tile(early, early, 0, free=early >= 3)
                        early += 1

            def transpose_max(g, buf, first=False):
                pe.wait_ge(max_all, g + 1)
                if not first:
                    pe.wait_ge(nm_all, g)
                pe.transpose(maxima_T, row_max[:, buf, :], ident_f[:]).then_inc(max_T, 1)

            def score_step(g, s, buf, first=False):
                qh, kt, pr = STEPS[s]
                q0 = q_from(qh, kt)
                n = (qh + 1) * HALF - q0
                diag = q0 == kt * P
                if s >= 2 or not first:
                    pe.wait_ge(exp_done, NST * g + s - 1)
                for a in range(2):
                    r = 2 * pr + a
                    bank = 2 * (s % 2) + a
                    mm = pe.matmul(ps[:, bank, 0:n], k_stack[buf][0:STACKM, kt * P:(kt + 1) * P],
                                   q_stack[buf][0:STACKM, r * T + q0:r * T + q0 + n], start=True, stop=not diag)
                    if diag:
                        mm = pe.matmul(ps[:, bank, 0:P], ident_b[:], mask_k[:], start=False, stop=True)
                mm.then_inc(st_ready, 1)

            def pv(g, m, buf):
                qh, kt, _ = STEPS[2 * m]
                off = q_from(qh, kt) - qh * HALF
                n = HALF - off
                pe.wait_ge(exp_done, NST * g + 2 * m + 2)
                if m == 0:
                    pe.wait_ge(ctx_evac, NH * g + FREE)
                if m == 4:
                    pe.wait_ge(ctx_evac, NH * g + 1 + FREE)
                for r in range(REP):
                    s = 2 * m + r // 2
                    mm = pe.matmul(ps[32 * r:32 * r + 32, B_CTX, off:HALF], v_ones[buf][:, kt, :],
                                   probs[:, s % 4, r % 2, 0:n], start=kt == 0, stop=kt == 4 * (qh + 1) - 1)
                mm.then_inc(pv_done, 1)

            for k in range(early, NMAX):
                max_tile(k, k, 0)
            pe.wait_ge(part_r, NKQ)
            pe.wait_ge(stack_in[1], 192)
            for k in range(LEAD):
                if k == 2:
                    pe.wait_ge(nm_r, 1)
                max_tile(NMAX + k, k, 1)
                if k == 1:
                    transpose_max(0, 0, first=True)

            def first_steps(g, c, first=False):
                pe.wait_ge(mrow_in, 48 * (g + 1))
                for s in range(2):
                    score_step(g, s, c, first)

            def group(g, it, c, count=NMAX, last=False):
                pe.wait_ge(v_staged, g + 1)
                for s in range(NST):
                    if s >= 2:
                        score_step(g, s, c)
                    for k in (2 * s, 2 * s + 1):
                        if k >= count:
                            continue
                        if k == NMAX - LEAD:
                            pe.wait_ge(stack_in[(c + 2) % 3], 192 * (it + (c + 2) // 3 + 1))
                        if k == NMAX - LEAD + 2:
                            pe.wait_ge(nm_r, g + 2)
                        max_tile(NMAX * (g + 1) + LEAD + k, (LEAD + k) % NMAX, (c + 1 + (LEAD + k) // NMAX) % 3)
                    if s == TR_STEP and count:
                        transpose_max(g + 1, (c + 1) % 3)
                    if s >= 3 and s % 2 == 1:
                        pv(g, (s - 3) // 2, c)
                if not last:
                    first_steps(g + 1, (c + 1) % 3)
                pv(g, NPV - 1, c)

            first_steps(0, 0, first=True)
            with pe.Fori(0, 2) as it:
                for c in range(3):
                    group(it * 3 + c, it, c)
            group(6, 2, 0, count=NMAX - LEAD)
            group(7, 2, 1, count=0, last=True)

            def wo_tile(tt, chunks):
                return three_pass(ps[:, tt, :], lambda c: ctx_hi[:, c, tt * P:(tt + 1) * P],
                                  lambda c: ctx_lo[:, c, tt * P:(tt + 1) * P], lambda c: wo_hi[:, c, :],
                                  lambda c: wo_lo[:, c, :], chunks, start=chunks[0] == 0, stop=chunks[-1] == KC - 1)

            def x1_transpose(tt):
                pe.wait_ge(ln_x, tt + 1)
                for c in range(KC):
                    mm = pe.transpose(ps[:, tt, c * P:(c + 1) * P], xres[:, tt, c * P:(c + 1) * P], ident_f[:])
                mm.then_inc(x1T_ps, 1)

            pe.wait_ge(wo_lo_s, 1)
            pe.wait_ge(ctx_lo_s, KC - 1)
            pe.wait_ge(exp_done, NST * G)
            pe.wait_ge(max_done, NMAX * G)
            pe.wait_ge(nm_all, G)
            for tt in range(TT):
                if tt == B_CTX:
                    pe.wait_ge(ctx_evac, NH * G + FREE)
                wo_tile(tt, range(KC - 1))
            pe.wait_ge(ctx_lo_s, KC)
            for tt in range(TT):
                wo_tile(tt, range(KC - 1, KC)).then_inc(attn_out, 1)

            def gate_or_up(par, which, hf):
                return three_pass(ps[:, 4 * par + 2 * which + hf, :],
                                  lambda c: gu_hi[:, par, which * UNIT + c * P:which * UNIT + (c + 1) * P],
                                  lambda c: gu_lo[:, par, which * UNIT + c * P:which * UNIT + (c + 1) * P],
                                  lambda c: x1T_hi[:, c, hf * HALF:(hf + 1) * HALF],
                                  lambda c: x1T_lo[:, c, hf * HALF:(hf + 1) * HALF], range(KC))

            for tt in range(4):
                x1_transpose(tt)
            for j in range(2):
                pe.wait_ge(gu_lo_s, j + 1)
                for which in range(2):
                    x1_transpose(4 + 2 * j + which)
                    pe.wait_ge(x1T_lo_s, (4, 4, 5, 7)[2 * j + which])
                    gate_or_up(j, which, 0)
            pe.wait_ge(x1T_lo_s, TT)
            for j in range(2):
                for which in range(2):
                    gate_or_up(j, which, 1).then_inc(gate_up, 1)
            with pe.Fori(2, MT - 1, 2) as j:
                for par in range(2):
                    pe.wait_ge(hid_s, j + par - 1)
                    pe.wait_ge(gu_lo_s, j + par + 1)
                    for which in range(2):
                        for hf in range(NH):
                            mm = gate_or_up(par, which, hf)
                        mm.then_inc(gate_up, 1)

            def down_tile(tt, par, first=False):
                for j in range(MT):
                    if first:
                        pe.wait_ge(wd_lo_s, j + 1)
                    if j == (MT - 1 if first and par == 0 else 0):
                        pe.wait_ge(hl_s, tt + 1)
                    for p3 in range(3):
                        a = (hid_hi, hid_hi, hid_lo)[p3][par][:, j, :]
                        b = wd_lo(j) if p3 == 1 else wd_hi[:, j, :]
                        mm = pe.matmul(ps[:, par, :], a, b, start=j == 0 and p3 == 0, stop=j == MT - 1 and p3 == 2)
                mm.then_inc(down, 1)

            pe.wait_ge(hid_s, MT - 1)
            pe.wait_ge(hl_first, 1)
            for par in range(2):
                down_tile(par, par, first=True)
            with pe.Fori(2, TT - 1, 2) as tt:
                for par in range(2):
                    pe.wait_ge(ln_y, tt + par + TT - 1)
                    down_tile(tt + par, par)


def kernel(L0_attn_x, L0_attn_Wq, L0_attn_Wkv, L0_attn_Wo, L0_attn_bo, L0_ffn_gate_q, L0_ffn_gate_absmax,
           L0_ffn_up_q, L0_ffn_up_absmax, L0_ffn_down_q, L0_ffn_down_absmax):
    import concourse.bacc as bacc
    from concourse.bass_utils import run_bass_kernel_spmd

    x = np.asarray(L0_attn_x)[0]
    wq = np.asarray(L0_attn_Wq).reshape(D, G, REP, HD).transpose(0, 1, 3, 2).reshape(D, D)
    wkv = np.asarray(L0_attn_Wkv).reshape(D, G, 2, HD).transpose(0, 2, 1, 3).reshape(D, 2 * G * HD)

    def wide(q):
        return np.asarray(q).reshape(MT, P, KC, P).transpose(0, 3, 2, 1).reshape(MT, P, UNIT)

    def wide_scale(a):
        return np.asarray(a).reshape(MT, P, KC, 2).transpose(0, 3, 2, 1).reshape(MT, 2, UNIT)

    gate_up = np.stack([wide(L0_ffn_gate_q), wide(L0_ffn_up_q)], 1).reshape(2 * MT, P, UNIT)
    gate_up_s = np.stack([wide_scale(L0_ffn_gate_absmax), wide_scale(L0_ffn_up_absmax)], 1).reshape(2 * MT, 2, UNIT)
    down = np.asarray(L0_ffn_down_q).T.reshape(MT, P, UNIT)
    down_s = np.asarray(L0_ffn_down_absmax).reshape(D, 2 * MT).T.reshape(MT, 2, UNIT)
    arrays = {
        "x": x, "xT": x.T, "w_qkv": np.concatenate([wq, wkv], 1), "wo": np.asarray(L0_attn_Wo),
        "bo": np.asarray(L0_attn_bo),
        "codes": np.concatenate([down, gate_up], 0), "scales": np.concatenate([down_s, gate_up_s], 0),
    }
    arrays = {k: np.ascontiguousarray(v) for k, v in arrays.items()}
    nc = bacc.Bacc("TRN2", target_bir_lowering=False, num_devices=1)
    t = {k: nc.dram_tensor(k, list(v.shape), mybir.dt.from_np(v.dtype), kind="ExternalInput").ap()
         for k, v in arrays.items()}
    t["q_scr"] = nc.dram_tensor("q_scr", [3, D, T], BF16, kind="Internal").ap()
    t["k_scr"] = nc.dram_tensor("k_scr", [3, P, T], BF16, kind="Internal").ap()
    t["ctx_scr"] = nc.dram_tensor("ctx_scr", [G, P, T], F32, kind="Internal").ap()
    t["rsum_scr"] = nc.dram_tensor("rsum_scr", [KC, 2 * REP, T], F32, kind="Internal").ap()
    t["out"] = nc.dram_tensor("out", [T, D], F32, kind="ExternalOutput").ap()
    build_program(nc, t)
    r = run_bass_kernel_spmd(nc, [arrays], core_ids=[0])
    return np.asarray(r.results[0]["out"]).reshape(1, T, D)
```
